# Optimizing a Trainium2 kernel written in Bass

```python
import numpy as np
import jax
import jax.numpy as jnp

def _softmax(x, axis=-1):
    return jax.nn.softmax(x, axis=axis)

def _gelu(x):
    return jax.nn.gelu(x, approximate=True)

def _silu(x):
    return jax.nn.silu(x)

def _sigmoid(x):
    return jax.nn.sigmoid(x)

def _layernorm(x, axis=-1, eps=1e-05):
    m = jnp.mean(x, axis=axis, keepdims=True)
    v = jnp.var(x, axis=axis, keepdims=True)
    return (x - m) / jnp.sqrt(v + eps)

def _scatter_add(tgt, idx, src, axis=0):
    return tgt.at[idx].add(src)

def _segment_sum(src, seg, n):
    return jax.ops.segment_sum(src, seg, n)
kernel_name = 'mk_dlrm_tower_d1_rec_r8_f8b1e9'

def setup_inputs(seed: int=0):
    np.random.seed(seed)
    _w = jnp.asarray

    def _rec_inputs():
        import jax
        import jax.numpy as jnp
        _tk = jax.random.key(seed)
        dense_ctx = jax.random.normal(jax.random.fold_in(_tk, 190), (512, 16), jnp.float32)
        ids = jnp.stack([jax.random.randint(jax.random.fold_in(_tk, 200 + f), (512,), 0, v, jnp.int32) for f, v in enumerate([1250, 1000, 125000, 125000, 1250, 1000, 1250, 1000, 125000, 1000, 12500, 1250, 125000, 125000, 12500, 1000, 125000, 1000, 12500, 125000, 1000, 1250, 125000, 1250, 1250, 125000, 1000, 12500, 1250, 12500, 125000, 1000, 12500, 12500, 12500, 1000, 125000, 125000, 125000, 12500, 1250, 12500, 1250, 1250, 12500, 1250, 1250, 1250, 1000, 1000])], axis=1)
        tbl_0 = 0.05 * jax.random.normal(jax.random.fold_in(_tk, 500 + 0), (1250, 16), jnp.float32)
        tbl_1 = 0.05 * jax.random.normal(jax.random.fold_in(_tk, 500 + 1), (1000, 16), jnp.float32)
        tbl_2 = 0.05 * jax.random.normal(jax.random.fold_in(_tk, 500 + 2), (125000, 16), jnp.float32)
        tbl_3 = 0.05 * jax.random.normal(jax.random.fold_in(_tk, 500 + 3), (125000, 16), jnp.float32)
        tbl_4 = 0.05 * jax.random.normal(jax.random.fold_in(_tk, 500 + 4), (1250, 16), jnp.float32)
        tbl_5 = 0.05 * jax.random.normal(jax.random.fold_in(_tk, 500 + 5), (1000, 16), jnp.float32)
        tbl_6 = 0.05 * jax.random.normal(jax.random.fold_in(_tk, 500 + 6), (1250, 16), jnp.float32)
        tbl_7 = 0.05 * jax.random.normal(jax.random.fold_in(_tk, 500 + 7), (1000, 16), jnp.float32)
        tbl_8 = 0.05 * jax.random.normal(jax.random.fold_in(_tk, 500 + 8), (125000, 16), jnp.float32)
        tbl_9 = 0.05 * jax.random.normal(jax.random.fold_in(_tk, 500 + 9), (1000, 16), jnp.float32)
        tbl_10 = 0.05 * jax.random.normal(jax.random.fold_in(_tk, 500 + 10), (12500, 16), jnp.float32)
        tbl_11 = 0.05 * jax.random.normal(jax.random.fold_in(_tk, 500 + 11), (1250, 16), jnp.float32)
        tbl_12 = 0.05 * jax.random.normal(jax.random.fold_in(_tk, 500 + 12), (125000, 16), jnp.float32)
        tbl_13 = 0.05 * jax.random.normal(jax.random.fold_in(_tk, 500 + 13), (125000, 16), jnp.float32)
        tbl_14 = 0.05 * jax.random.normal(jax.random.fold_in(_tk, 500 + 14), (12500, 16), jnp.float32)
        tbl_15 = 0.05 * jax.random.normal(jax.random.fold_in(_tk, 500 + 15), (1000, 16), jnp.float32)
        tbl_16 = 0.05 * jax.random.normal(jax.random.fold_in(_tk, 500 + 16), (125000, 16), jnp.float32)
        tbl_17 = 0.05 * jax.random.normal(jax.random.fold_in(_tk, 500 + 17), (1000, 16), jnp.float32)
        tbl_18 = 0.05 * jax.random.normal(jax.random.fold_in(_tk, 500 + 18), (12500, 16), jnp.float32)
        tbl_19 = 0.05 * jax.random.normal(jax.random.fold_in(_tk, 500 + 19), (125000, 16), jnp.float32)
        tbl_20 = 0.05 * jax.random.normal(jax.random.fold_in(_tk, 500 + 20), (1000, 16), jnp.float32)
        tbl_21 = 0.05 * jax.random.normal(jax.random.fold_in(_tk, 500 + 21), (1250, 16), jnp.float32)
        tbl_22 = 0.05 * jax.random.normal(jax.random.fold_in(_tk, 500 + 22), (125000, 16), jnp.float32)
        tbl_23 = 0.05 * jax.random.normal(jax.random.fold_in(_tk, 500 + 23), (1250, 16), jnp.float32)
        tbl_24 = 0.05 * jax.random.normal(jax.random.fold_in(_tk, 500 + 24), (1250, 16), jnp.float32)
        tbl_25 = 0.05 * jax.random.normal(jax.random.fold_in(_tk, 500 + 25), (125000, 16), jnp.float32)
        tbl_26 = 0.05 * jax.random.normal(jax.random.fold_in(_tk, 500 + 26), (1000, 16), jnp.float32)
        tbl_27 = 0.05 * jax.random.normal(jax.random.fold_in(_tk, 500 + 27), (12500, 16), jnp.float32)
        tbl_28 = 0.05 * jax.random.normal(jax.random.fold_in(_tk, 500 + 28), (1250, 16), jnp.float32)
        tbl_29 = 0.05 * jax.random.normal(jax.random.fold_in(_tk, 500 + 29), (12500, 16), jnp.float32)
        tbl_30 = 0.05 * jax.random.normal(jax.random.fold_in(_tk, 500 + 30), (125000, 16), jnp.float32)
        tbl_31 = 0.05 * jax.random.normal(jax.random.fold_in(_tk, 500 + 31), (1000, 16), jnp.float32)
        tbl_32 = 0.05 * jax.random.normal(jax.random.fold_in(_tk, 500 + 32), (12500, 16), jnp.float32)
        tbl_33 = 0.05 * jax.random.normal(jax.random.fold_in(_tk, 500 + 33), (12500, 16), jnp.float32)
        tbl_34 = 0.05 * jax.random.normal(jax.random.fold_in(_tk, 500 + 34), (12500, 16), jnp.float32)
        tbl_35 = 0.05 * jax.random.normal(jax.random.fold_in(_tk, 500 + 35), (1000, 16), jnp.float32)
        tbl_36 = 0.05 * jax.random.normal(jax.random.fold_in(_tk, 500 + 36), (125000, 16), jnp.float32)
        tbl_37 = 0.05 * jax.random.normal(jax.random.fold_in(_tk, 500 + 37), (125000, 16), jnp.float32)
        tbl_38 = 0.05 * jax.random.normal(jax.random.fold_in(_tk, 500 + 38), (125000, 16), jnp.float32)
        tbl_39 = 0.05 * jax.random.normal(jax.random.fold_in(_tk, 500 + 39), (12500, 16), jnp.float32)
        tbl_40 = 0.05 * jax.random.normal(jax.random.fold_in(_tk, 500 + 40), (1250, 16), jnp.float32)
        tbl_41 = 0.05 * jax.random.normal(jax.random.fold_in(_tk, 500 + 41), (12500, 16), jnp.float32)
        tbl_42 = 0.05 * jax.random.normal(jax.random.fold_in(_tk, 500 + 42), (1250, 16), jnp.float32)
        tbl_43 = 0.05 * jax.random.normal(jax.random.fold_in(_tk, 500 + 43), (1250, 16), jnp.float32)
        tbl_44 = 0.05 * jax.random.normal(jax.random.fold_in(_tk, 500 + 44), (12500, 16), jnp.float32)
        tbl_45 = 0.05 * jax.random.normal(jax.random.fold_in(_tk, 500 + 45), (1250, 16), jnp.float32)
        tbl_46 = 0.05 * jax.random.normal(jax.random.fold_in(_tk, 500 + 46), (1250, 16), jnp.float32)
        tbl_47 = 0.05 * jax.random.normal(jax.random.fold_in(_tk, 500 + 47), (1250, 16), jnp.float32)
        tbl_48 = 0.05 * jax.random.normal(jax.random.fold_in(_tk, 500 + 48), (1000, 16), jnp.float32)
        tbl_49 = 0.05 * jax.random.normal(jax.random.fold_in(_tk, 500 + 49), (1000, 16), jnp.float32)
        _rk = jax.random.fold_in(_tk, 7)
        W_top1 = 0.0283866 * jax.random.normal(jax.random.fold_in(_tk, 801), (1241, 512), jnp.float32)
        W_top2 = 0.0441942 * jax.random.normal(jax.random.fold_in(_tk, 802), (512, 256), jnp.float32)
        W_top3 = 0.0625 * jax.random.normal(jax.random.fold_in(_tk, 803), (256, 1), jnp.float32)
        b_top1 = jnp.zeros((512,), jnp.float32)
        b_top2 = jnp.zeros((256,), jnp.float32)
        return (dense_ctx, ids, tbl_0, tbl_1, tbl_2, tbl_3, tbl_4, tbl_5, tbl_6, tbl_7, tbl_8, tbl_9, tbl_10, tbl_11, tbl_12, tbl_13, tbl_14, tbl_15, tbl_16, tbl_17, tbl_18, tbl_19, tbl_20, tbl_21, tbl_22, tbl_23, tbl_24, tbl_25, tbl_26, tbl_27, tbl_28, tbl_29, tbl_30, tbl_31, tbl_32, tbl_33, tbl_34, tbl_35, tbl_36, tbl_37, tbl_38, tbl_39, tbl_40, tbl_41, tbl_42, tbl_43, tbl_44, tbl_45, tbl_46, tbl_47, tbl_48, tbl_49, W_top1, b_top1, W_top2, b_top2, W_top3)
    dense_ctx, ids, tbl_0, tbl_1, tbl_2, tbl_3, tbl_4, tbl_5, tbl_6, tbl_7, tbl_8, tbl_9, tbl_10, tbl_11, tbl_12, tbl_13, tbl_14, tbl_15, tbl_16, tbl_17, tbl_18, tbl_19, tbl_20, tbl_21, tbl_22, tbl_23, tbl_24, tbl_25, tbl_26, tbl_27, tbl_28, tbl_29, tbl_30, tbl_31, tbl_32, tbl_33, tbl_34, tbl_35, tbl_36, tbl_37, tbl_38, tbl_39, tbl_40, tbl_41, tbl_42, tbl_43, tbl_44, tbl_45, tbl_46, tbl_47, tbl_48, tbl_49, W_top1, b_top1, W_top2, b_top2, W_top3 = _rec_inputs()

    def _L0_rec_setup():
        import jax, jax.numpy as jnp
        import numpy as np
        _NUM_FIELDS = 50
        _I_IDX, _J_IDX = np.triu_indices(_NUM_FIELDS, k=1)
        key = jax.random.key(seed)
        x = jax.random.normal(key, (2048, _NUM_FIELDS, 16), dtype=jnp.float32)
        return {'x': x}
    _L0_rec_all = _L0_rec_setup()
    _L0_rec_in = {k: v for k, v in _L0_rec_all.items() if k in ()}
    del _L0_rec_all
    return {'dense_ctx': dense_ctx, 'ids': ids, 'tbl_0': tbl_0, 'tbl_1': tbl_1, 'tbl_2': tbl_2, 'tbl_3': tbl_3, 'tbl_4': tbl_4, 'tbl_5': tbl_5, 'tbl_6': tbl_6, 'tbl_7': tbl_7, 'tbl_8': tbl_8, 'tbl_9': tbl_9, 'tbl_10': tbl_10, 'tbl_11': tbl_11, 'tbl_12': tbl_12, 'tbl_13': tbl_13, 'tbl_14': tbl_14, 'tbl_15': tbl_15, 'tbl_16': tbl_16, 'tbl_17': tbl_17, 'tbl_18': tbl_18, 'tbl_19': tbl_19, 'tbl_20': tbl_20, 'tbl_21': tbl_21, 'tbl_22': tbl_22, 'tbl_23': tbl_23, 'tbl_24': tbl_24, 'tbl_25': tbl_25, 'tbl_26': tbl_26, 'tbl_27': tbl_27, 'tbl_28': tbl_28, 'tbl_29': tbl_29, 'tbl_30': tbl_30, 'tbl_31': tbl_31, 'tbl_32': tbl_32, 'tbl_33': tbl_33, 'tbl_34': tbl_34, 'tbl_35': tbl_35, 'tbl_36': tbl_36, 'tbl_37': tbl_37, 'tbl_38': tbl_38, 'tbl_39': tbl_39, 'tbl_40': tbl_40, 'tbl_41': tbl_41, 'tbl_42': tbl_42, 'tbl_43': tbl_43, 'tbl_44': tbl_44, 'tbl_45': tbl_45, 'tbl_46': tbl_46, 'tbl_47': tbl_47, 'tbl_48': tbl_48, 'tbl_49': tbl_49, 'W_top1': W_top1, 'b_top1': b_top1, 'W_top2': W_top2, 'b_top2': b_top2, 'W_top3': W_top3}

def reference(dense_ctx, ids, tbl_0, tbl_1, tbl_2, tbl_3, tbl_4, tbl_5, tbl_6, tbl_7, tbl_8, tbl_9, tbl_10, tbl_11, tbl_12, tbl_13, tbl_14, tbl_15, tbl_16, tbl_17, tbl_18, tbl_19, tbl_20, tbl_21, tbl_22, tbl_23, tbl_24, tbl_25, tbl_26, tbl_27, tbl_28, tbl_29, tbl_30, tbl_31, tbl_32, tbl_33, tbl_34, tbl_35, tbl_36, tbl_37, tbl_38, tbl_39, tbl_40, tbl_41, tbl_42, tbl_43, tbl_44, tbl_45, tbl_46, tbl_47, tbl_48, tbl_49, W_top1, b_top1, W_top2, b_top2, W_top3):
    import jax
    import jax.numpy as jnp

    def _L0_rec_ref(x):
        import jax, jax.numpy as jnp
        import numpy as np
        _NUM_FIELDS = 50
        _I_IDX, _J_IDX = np.triu_indices(_NUM_FIELDS, k=1)
        gram = jnp.einsum('bid,bjd->bij', x, x)
        return gram[:, _I_IDX, _J_IDX]
    e = jnp.stack([tbl_0[ids[:, 0]], tbl_1[ids[:, 1]], tbl_2[ids[:, 2]], tbl_3[ids[:, 3]], tbl_4[ids[:, 4]], tbl_5[ids[:, 5]], tbl_6[ids[:, 6]], tbl_7[ids[:, 7]], tbl_8[ids[:, 8]], tbl_9[ids[:, 9]], tbl_10[ids[:, 10]], tbl_11[ids[:, 11]], tbl_12[ids[:, 12]], tbl_13[ids[:, 13]], tbl_14[ids[:, 14]], tbl_15[ids[:, 15]], tbl_16[ids[:, 16]], tbl_17[ids[:, 17]], tbl_18[ids[:, 18]], tbl_19[ids[:, 19]], tbl_20[ids[:, 20]], tbl_21[ids[:, 21]], tbl_22[ids[:, 22]], tbl_23[ids[:, 23]], tbl_24[ids[:, 24]], tbl_25[ids[:, 25]], tbl_26[ids[:, 26]], tbl_27[ids[:, 27]], tbl_28[ids[:, 28]], tbl_29[ids[:, 29]], tbl_30[ids[:, 30]], tbl_31[ids[:, 31]], tbl_32[ids[:, 32]], tbl_33[ids[:, 33]], tbl_34[ids[:, 34]], tbl_35[ids[:, 35]], tbl_36[ids[:, 36]], tbl_37[ids[:, 37]], tbl_38[ids[:, 38]], tbl_39[ids[:, 39]], tbl_40[ids[:, 40]], tbl_41[ids[:, 41]], tbl_42[ids[:, 42]], tbl_43[ids[:, 43]], tbl_44[ids[:, 44]], tbl_45[ids[:, 45]], tbl_46[ids[:, 46]], tbl_47[ids[:, 47]], tbl_48[ids[:, 48]], tbl_49[ids[:, 49]]], axis=1)
    z = _L0_rec_ref(e)
    z = z.reshape(z.shape[0], -1)
    h = jnp.concatenate([z, dense_ctx], axis=1)
    h = jnp.maximum(h @ W_top1 + b_top1, 0.0)
    h = jnp.maximum(h @ W_top2 + b_top2, 0.0)
    y = h @ W_top3
    return y

_drawn_inputs = setup_inputs


def setup_inputs(seed=0):
    import zlib

    import numpy as np

    out = dict(_drawn_inputs(seed))
    spreads = {'b_top1': (0.0, 0.1), 'b_top2': (0.0, 0.1)}
    factors = {'tbl_0': 5.13,
     'tbl_1': 5.061,
     'tbl_2': 4.221,
     'tbl_3': 4.486,
     'tbl_4': 4.085,
     'tbl_5': 4.774,
     'tbl_6': 4.427,
     'tbl_7': 4.308,
     'tbl_8': 4.889,
     'tbl_9': 4.574,
     'tbl_10': 4.596,
     'tbl_11': 4.637,
     'tbl_12': 4.364,
     'tbl_13': 4.296,
     'tbl_14': 4.35,
     'tbl_15': 4.396,
     'tbl_16': 5.224,
     'tbl_17': 4.528,
     'tbl_18': 4.871,
     'tbl_19': 4.985,
     'tbl_20': 4.469,
     'tbl_21': 4.611,
     'tbl_22': 4.906,
     'tbl_23': 4.81,
     'tbl_24': 4.66,
     'tbl_25': 4.732,
     'tbl_26': 4.729,
     'tbl_27': 5.081,
     'tbl_28': 4.82,
     'tbl_29': 4.872,
     'tbl_30': 4.892,
     'tbl_31': 5.635,
     'tbl_32': 4.716,
     'tbl_33': 5.016,
     'tbl_34': 5.505,
     'tbl_35': 4.528,
     'tbl_36': 4.685,
     'tbl_37': 4.58,
     'tbl_38': 4.507,
     'tbl_39': 4.288,
     'tbl_40': 4.394,
     'tbl_41': 4.72,
     'tbl_42': 4.435,
     'tbl_43': 4.634,
     'tbl_44': 4.763,
     'tbl_45': 4.579,
     'tbl_46': 4.737,
     'tbl_47': 4.239,
     'tbl_48': 4.576,
     'tbl_49': 4.592}
    for name, (base, spread) in spreads.items():
        noise = np.random.default_rng([zlib.crc32(name.encode()), seed]).standard_normal(out[name].shape)
        drawn = base * np.exp(spread * noise) if base else spread * noise
        out[name] = jnp.asarray(drawn.astype(out[name].dtype))
    for name, factor in factors.items():
        out[name] = (out[name] * factor).astype(out[name].dtype)
    return out
```

```python
import concourse.bass as bass
from concourse import mybir
from contextlib import ExitStack

BATCH = 512
FIELDS = 50
DIM = 16
P = 128
TILES = BATCH // P
HIDDEN1, HIDDEN2 = 512, 256
ROWS = [1250, 1000, 125000, 125000, 1250, 1000, 1250, 1000, 125000, 1000, 12500, 1250, 125000, 125000, 12500,
        1000, 125000, 1000, 12500, 125000, 1000, 1250, 125000, 1250, 1250, 125000, 1000, 12500, 1250, 12500,
        125000, 1000, 12500, 12500, 12500, 1000, 125000, 125000, 125000, 12500, 1250, 12500, 1250, 1250, 12500,
        1250, 1250, 1250, 1000, 1000]

HI = 125
SMALL = [f for f in range(FIELDS) if ROWS[f] == 1250] + [f for f in range(FIELDS) if ROWS[f] == 1000]
BIG = [f for f in range(FIELDS) if ROWS[f] > 1250]
ORDER = SMALL + BIG
NS, NB = len(SMALL), len(BIG)
PAIRS = NS // 2
LO = [ROWS[f] // HI for f in SMALL]
LO_AT = [sum(LO[:s]) for s in range(NS + 1)]
PARTS = 3
K3 = PARTS * DIM
LEFT = [0, 1, 2, 0, 0, 1]
RIGHT = [0, 1, 0, 2, 1, 0]
KG = DIM * len(LEFT)

G12 = 12
SLOTS = 12
RECT_AT = {1: 0, 2: 12, 3: 36}
TRI_AT = 72
LAST_AT = 116
DENSE_AT, DENSE_SLOT = 72, 11
FINAL_AT = 88
SLOT_ROWS = [128] * 8 + [116] * 3 + [FINAL_AT + 1]

SPF = 8
FILLS = P // SPF
OH_RING = 8
ID_RING = 3
SPLIT_CHUNKS = [(0, 2), (2, 5), (5, 9), (9, PAIRS)]


def dlrm_tower(nc, a, out):
    f32, bf16, fp16, i32 = mybir.dt.float32, mybir.dt.bfloat16, mybir.dt.float16, mybir.dt.int32
    ALU = mybir.AluOpType
    ACT = mybir.ActivationFunctionType
    ctx = ExitStack()
    with ctx:
        def sb(name, shape, dt):
            return ctx.enter_context(nc.sbuf_tensor(name, shape, dt))

        def pb(name, shape, dt):
            return ctx.enter_context(nc.psum_tensor(name, shape, dt))

        def sem(name):
            return ctx.enter_context(nc.semaphore(name))

        id_scratch = nc.dram_tensor("id_scratch", (NS, BATCH), fp16, kind="Internal").ap()

        ids = sb("ids", [P, TILES, FIELDS], i32)
        ids_h = sb("ids_h", [P, TILES, NS], fp16)
        id_rows = sb("id_rows", [NS, BATCH], fp16)
        id_all = sb("id_all", [HI, ID_RING, 2, BATCH], fp16)
        iota_i = sb("iota_i", [HI, 18], i32)
        iota_f = sb("iota_f", [HI, 18], f32)
        ident = sb("ident", [P, P], f32)
        ident_b = sb("ident_b", [P, P], bf16)
        ident_h = sb("ident_h", [P, P], fp16)
        gram_mem = sb("gram_mem", [P, FIELDS * P], f32)
        gram = gram_mem[0:FIELDS, :].rearrange("i (j b) -> i j b", b=P)
        tbl = gram_mem[0:HI, 0:LO_AT[NS] * DIM].rearrange("p (l d) -> p l d", d=DIM)
        w1 = sb("w1", [P, SLOTS, HIDDEN1], f32)
        tbl3 = w1[0:HI, :, :].rearrange("p s n -> p (s n)")[:, 0:LO_AT[NS] * K3 // 2].bitcast(bf16)
        tbl3 = tbl3.rearrange("p (l k) -> p l k", k=K3)
        onehot = sb("onehot", [HI, OH_RING, BATCH], bf16)
        emb = sb("emb", [P, 2, NB, DIM], f32)
        emb3 = sb("emb3", [P, 2, NB, K3], bf16)
        lhs = sb("lhs", [KG, TILES, FIELDS, P], bf16)
        rhs = sb("rhs", [KG, TILES, FIELDS, P], bf16)
        z = sb("z", [P, SLOTS, P], f32)
        dense = sb("dense", [P, TILES, DIM], f32)
        dense_t = sb("dense_t", [DIM, BATCH], f32)
        w2 = sb("w2", [P, HIDDEN1 // P, HIDDEN2], f32)
        vec = sb("vec", [8, P], f32)
        vec_t = sb("vec_t", [P, 8], f32)
        h1 = sb("h1", [P, HIDDEN1 // P, P], f32)
        h2 = sb("h2", [P, HIDDEN2 // P, P], f32)
        y = sb("y", [P, TILES], f32)

        ps_look = [pb(f"ps_look{i}", [P, BATCH], f32) for i in range(2)]
        ps_tr = [pb(f"ps_tr{i}", [P, 1024], bf16) for i in range(2)]
        ps_gram = [pb(f"ps_gram{i}", [P, SPF, 64], f32) for i in range(2)]
        ps_h1 = pb("ps_h1", [P, HIDDEN1 // P, P], f32)
        ps_h2 = pb("ps_h2", [P, 512], f32)
        ps_ids = ps_tr[0][0:NS, 0:BATCH].bitcast(fp16)
        ps_dense = ps_h1[0:DIM, :, :]
        ps_vec = ps_h2[:, 0:8]

        ids_in = sem("ids_in")
        tbl_in = [sem(f"tbl_in{c}") for c in range(len(SPLIT_CHUNKS))]
        w1_in, w2_in, vec_in, dense_in = sem("w1_in"), sem("w2_in"), sem("vec_in"), sem("dense_in")
        ident_zero, ident_ok, ident_b_ok = sem("ident_zero"), sem("ident_ok"), sem("ident_b_ok")
        ident_h_ok = sem("ident_h_ok")
        iota_ok, iota_f_ok = sem("iota_ok"), sem("iota_f_ok")
        ids_h_ok, ids_turned, id_rows_ok = sem("ids_h_ok"), sem("ids_turned"), sem("id_rows_ok")
        id_scratch_ok = sem("id_scratch_ok")
        id_all_in = [sem(f"id_all_in{i}") for i in range(ID_RING)]
        pair_compared = sem("pair_compared")
        high_ok, rest_ok, mid_ok, tbl3_ok = sem("high_ok"), sem("rest_ok"), sem("mid_ok"), sem("tbl3_ok")
        onehot_ok, onehot_used = sem("onehot_ok"), sem("onehot_used")
        looked_up, look_copied = sem("looked_up"), sem("look_copied")
        rows_in = [sem(f"rows_in{t}") for t in range(TILES)]
        e_high, e_rest, e_mid, emb3_ok = sem("e_high"), sem("e_rest"), sem("e_mid"), sem("emb3_ok")
        turned, turned_copied = sem("turned"), sem("turned_copied")
        small_ops = [sem(f"small_ops{i}") for i in range(2)]
        big_ops = [sem(f"big_ops{i}") for i in range(TILES)]
        gram_ok = sem("gram_ok")
        gram_out_act, gram_out_dve = sem("gram_out_act"), sem("gram_out_dve")
        z_in = sem("z_in")
        dense_turned, dense_t_ok, vec_turned, vec_t_ok = (sem("dense_turned"), sem("dense_t_ok"),
                                                          sem("vec_turned"), sem("vec_t_ok"))
        layer1, h1_ok, layer2, h2_ok = sem("layer1"), sem("h1_ok"), sem("layer2"), sem("h2_ok")
        layer3, y_ok, out_ok = sem("layer3"), sem("y_ok"), sem("out_ok")

        moves = [(RECT_AT[g], 12 * g, 0, 12, 0, 12 * g) for g in (1, 2, 3)]
        moves += [(TRI_AT + 11 * g, 11, 0, 11, 12 * g, 12 * g + 1) for g in range(4)]
        moves += [(LAST_AT, 12, 2 * q, 2, 12 * q, 48) for q in range(4)]
        moves += [(FINAL_AT, 1, DENSE_SLOT, 1, 48, 49)]
        Z_COUNT = 16 * (len(moves) + 1)

        copies = [(0, 48, 0, 16), (0, 64, 0, 32), (1, 0, 0, 32), (1, 32, 0, 16), (1, 48, 32, 16),
                  (1, 64, 16, 16), (1, 80, 0, 16)]
        OPS_COUNT = 16 * len(copies)

        block = ctx.enter_context(nc.Block())

        @block.sync
        def _(sp):
            sp.dma_start(ids[:, :, :], a["ids"].rearrange("(p t) f -> p t f", t=TILES)).then_inc(ids_in, 16)
            sp.dma_start(vec[0:4, :], a["b_top1"].rearrange("(c p) -> c p", p=P)).then_inc(vec_in, 16)
            sp.dma_start(vec[4:6, :], a["b_top2"].rearrange("(c p) -> c p", p=P)).then_inc(vec_in, 16)
            sp.dma_start(vec[6:8, :], a["W_top3"].rearrange("(c p) n -> c (p n)", p=P)).then_inc(vec_in, 16)
            sp.dma_start(dense[:, :, :], a["dense_ctx"].rearrange("(p t) d -> p t d", t=TILES)).then_inc(dense_in, 16)
            sp.wait_ge(id_rows_ok, 1)
            sp.dma_start(id_scratch, id_rows[:, :]).then_inc(id_scratch_ok, 16)
            sp.wait_ge(id_scratch_ok, 16)
            for q in range(PAIRS):
                if q >= ID_RING:
                    sp.wait_ge(pair_compared, q - ID_RING + 1)
                src = id_scratch[2 * q:2 * q + 2, :].rearrange("(o f) b -> o f b", o=1).broadcast_to((HI, 2, BATCH))
                sp.dma_start(id_all[:, q % ID_RING, :, :], src).then_inc(id_all_in[q % ID_RING], 16)
                if q == 4:
                    sp.dma_start(w2[:, :, :], a["W_top2"].rearrange("(c p) n -> p c n", p=P)).then_inc(w2_in, 16)

            def spread(tiles, fields, done):
                for side, row, src, rows in copies:
                    dst = (lhs, rhs)[side]
                    sp.dma_start(dst[row:row + rows, tiles, fields, :],
                                 lhs[src:src + rows, tiles, fields, :]).then_inc(done, 16)

            def spread_big(t):
                sp.wait_ge(turned_copied, 3 * (t + 1))
                spread(slice(t, t + 1), slice(NS, FIELDS), big_ops[t])

            def fill_z(t):
                if t >= 1:
                    sp.wait_ge(layer1, t)
                sp.dma_start(z[DENSE_AT:DENSE_AT + DIM, DENSE_SLOT, :], dense_t[:, t * P:(t + 1) * P]).then_inc(z_in, 16)
                sp.wait_ge(gram_out_act, FILLS // 2 * (t + 1))
                sp.wait_ge(gram_out_dve, FILLS // 2 * (t + 1))
                for row, rows, slot, slots, i, j in moves:
                    sp.dma_start(z[row:row + rows, slot:slot + slots, :], gram[i:i + rows, j:j + slots, :]).then_inc(z_in, 16)

            spread_big(0)
            sp.wait_ge(look_copied, NS)
            spread(slice(0, 1), slice(0, NS), small_ops[0])
            for s in range(0, SLOTS, 4):
                sp.dma_start(w1[:, s:s + 4, :], a["w1_slots"][:, s:s + 4, :]).then_inc(w1_in, 16)
            spread(slice(1, TILES), slice(0, NS), small_ops[1])
            sp.wait_ge(dense_t_ok, 1)
            spread_big(1)
            fill_z(0)
            fill_z(1)
            for t in range(2, TILES):
                spread_big(t)
                fill_z(t)
            sp.wait_ge(y_ok, TILES)
            sp.dma_start(out.rearrange("(p t) o -> p (t o)", t=TILES), y[:, :]).then_inc(out_ok, 16)
            sp.wait_ge(out_ok, 16)

        @block.gpsimd
        def _(pool):
            pool.memset(ident[:, :], 0.0).then_inc(ident_zero, 1)
            pool.iota(iota_i[:, 0:10], pattern=[[1, 10]], base=0, channel_multiplier=10)
            pool.iota(iota_i[:, 10:18], pattern=[[1, 8]], base=0, channel_multiplier=8).then_inc(iota_ok, 1)
            pool.wait_ge(ident_zero, 1)
            pool.affine_select(out=ident[:, :], in_=ident[:, :], compare_op=ALU.not_equal, fill=1.0, base=0,
                               pattern=[[-1, P]], channel_multiplier=1).then_inc(ident_ok, 1)
            pool.wait_ge(ids_in, 16)
            for t in range(TILES):
                if t >= 2:
                    pool.wait_ge(emb3_ok, t - 1)
                for k, f in enumerate(BIG):
                    pool.indirect_dma_start(
                        out=emb[:, t % 2, k, :], out_offset=None, in_=a[f"tbl_{f}"],
                        in_offset=bass.IndirectOffsetOnAxis(ap=ids[:, t, NS + k:NS + k + 1], axis=0),
                    ).then_inc(rows_in[t], 16)

        @block.scalar
        def _(act):
            for c, (q0, q1) in enumerate(SPLIT_CHUNKS):
                for s in range(2 * q0, 2 * q1):
                    act.dma_start(tbl[:, LO_AT[s]:LO_AT[s + 1], :],
                                  a[f"tbl_{SMALL[s]}"].rearrange("(p l) d -> p l d", l=LO[s])).then_inc(tbl_in[c], 16)
            def split_tables(c):
                q0, q1 = SPLIT_CHUNKS[c]
                at = slice(LO_AT[2 * q0], LO_AT[2 * q1])
                act.wait_ge(tbl_in[c], 32 * (q1 - q0))
                act.activation(tbl3[:, at, 0:DIM], tbl[:, at, :], ACT.Copy).then_inc(high_ok, 1)
                act.wait_ge(rest_ok, c + 1)
                act.activation(tbl3[:, at, DIM:2 * DIM], tbl[:, at, :], ACT.Copy).then_inc(mid_ok, 1)

            def copy_looked(q):
                act.wait_ge(looked_up, q + 1)
                for e in range(2):
                    act.activation(lhs[0:K3, :, 2 * q + e, :],
                                   ps_look[q % 2][64 * e:64 * e + K3, :].rearrange("k (t p) -> k t p", p=P),
                                   ACT.Copy).then_inc(look_copied, 1)

            def copy_turned(t):
                for g in range(3):
                    n = 3 * t + g
                    act.wait_ge(turned, n + 1)
                    act.activation(lhs[0:K3, t, NS + 8 * g:NS + 8 * g + 8, :],
                                   ps_tr[n % 2][0:K3, :].rearrange("k (f b) -> k f b", f=8),
                                   ACT.Copy).then_inc(turned_copied, 1)

            def gram_out(t):
                if t >= 1:
                    act.wait_ge(z_in, Z_COUNT * t)
                for k in range(1, FILLS, 2):
                    act.wait_ge(gram_ok, FILLS * t + k + 1)
                    act.activation(gram[:, :, SPF * k:SPF * k + SPF],
                                   ps_gram[k % 2][0:FIELDS, :, 0:FIELDS].rearrange("i b j -> i j b"),
                                   ACT.Copy).then_inc(gram_out_act, 1)

            split_tables(0)
            for q in range(PAIRS):
                for c in range(1, len(SPLIT_CHUNKS)):
                    if q == SPLIT_CHUNKS[c][0] - 2:
                        split_tables(c)
                copy_looked(q)
                if q == 8:
                    copy_turned(0)
            copy_turned(1)
            gram_out(0)
            gram_out(1)
            for t in range(2, TILES):
                copy_turned(t)
                gram_out(t)

        @block.vector
        def _(dve):
            dve.wait_ge(ident_ok, 1)
            dve.tensor_copy(ident_h[:, :], ident[:, :]).then_inc(ident_h_ok, 1)
            dve.wait_ge(ids_in, 16)
            dve.tensor_copy(ids_h[:, :, :], ids[:, :, 0:NS]).then_inc(ids_h_ok, 1)
            dve.tensor_copy(ident_b[:, :], ident[:, :]).then_inc(ident_b_ok, 1)
            dve.wait_ge(iota_ok, 1)
            dve.tensor_copy(iota_f[:, :], iota_i[:, :]).then_inc(iota_f_ok, 1)
            dve.wait_ge(ids_turned, 1)
            dve.tensor_copy(id_rows[:, :], ps_ids).then_inc(id_rows_ok, 1)
            dve.wait_ge(dense_turned, 1)
            dve.tensor_copy(dense_t[:, :].rearrange("d (t p) -> d t p", p=P), ps_dense).then_inc(dense_t_ok, 1)
            dve.wait_ge(vec_turned, 1)
            dve.tensor_copy(vec_t[:, :], ps_vec).then_inc(vec_t_ok, 1)

            def split_tables(c):
                q0, q1 = SPLIT_CHUNKS[c]
                at = slice(LO_AT[2 * q0], LO_AT[2 * q1])
                dve.wait_ge(high_ok, c + 1)
                dve.tensor_tensor(tbl[:, at, :], tbl[:, at, :], tbl3[:, at, 0:DIM], ALU.subtract).then_inc(rest_ok, 1)
                dve.wait_ge(mid_ok, c + 1)
                dve.tensor_tensor(tbl3[:, at, 2 * DIM:K3], tbl[:, at, :], tbl3[:, at, DIM:2 * DIM],
                                  ALU.subtract).then_inc(tbl3_ok, 1)

            def split_rows(t):
                e, e3 = emb[:, t % 2, :, :], emb3[:, t % 2, :, :]
                dve.wait_ge(rows_in[t], 16 * NB)
                if t >= 2:
                    dve.wait_ge(turned, 3 * (t - 1))
                dve.tensor_copy(e3[:, :, 0:DIM], e).then_inc(e_high, 1)
                dve.wait_ge(e_high, t + 1)
                dve.tensor_tensor(e, e, e3[:, :, 0:DIM], ALU.subtract).then_inc(e_rest, 1)
                dve.wait_ge(e_rest, t + 1)
                dve.tensor_copy(e3[:, :, DIM:2 * DIM], e).then_inc(e_mid, 1)
                dve.wait_ge(e_mid, t + 1)
                dve.tensor_tensor(e3[:, :, 2 * DIM:K3], e, e3[:, :, DIM:2 * DIM], ALU.subtract).then_inc(emb3_ok, 1)

            n = 0
            dve.wait_ge(iota_f_ok, 1)
            split_tables(0)
            for q in range(PAIRS):
                for c in range(1, len(SPLIT_CHUNKS)):
                    if q == SPLIT_CHUNKS[c][0] - 1:
                        split_tables(c)
                dve.wait_ge(id_all_in[q % ID_RING], 16 * (q // ID_RING + 1))
                base = 0 if LO[2 * q] == 10 else 10
                for lo in range(LO[2 * q]):
                    for e in range(2):
                        if n >= OH_RING:
                            dve.wait_ge(onehot_used, n - OH_RING + 1)
                        last = dve.tensor_scalar(onehot[:, n % OH_RING, :], id_all[:, q % ID_RING, e, :],
                                                 iota_f[:, base + lo:base + lo + 1], None, ALU.is_equal)
                        last.then_inc(onehot_ok, 1)
                        n += 1
                dve.wait_ge(onehot_ok, n)
                dve.sem_inc(pair_compared, 1)
                if q == 7:
                    split_rows(0)
            split_rows(1)

            def gram_out(t):
                if t >= 1:
                    dve.wait_ge(z_in, Z_COUNT * t)
                for k in range(0, FILLS, 2):
                    dve.wait_ge(gram_ok, FILLS * t + k + 1)
                    dve.tensor_copy(gram[:, :, SPF * k:SPF * k + SPF],
                                    ps_gram[k % 2][0:FIELDS, :, 0:FIELDS].rearrange("i b j -> i j b")
                                    ).then_inc(gram_out_dve, 1)

            def relu1(t):
                dve.wait_ge(layer1, t + 1)
                if t >= 1:
                    dve.wait_ge(layer2, t)
                for c in range(HIDDEN1 // P):
                    dve.tensor_scalar(h1[:, c, :], ps_h1[:, c, :], vec_t[:, c:c + 1], 0.0, ALU.add, ALU.max
                                      ).then_inc(h1_ok, 1)

            def relu2(t):
                dve.wait_ge(layer2, t + 1)
                if t >= 1:
                    dve.wait_ge(layer3, t)
                for c in range(HIDDEN2 // P):
                    dve.tensor_scalar(h2[:, c, :], ps_h2[:, c * P:(c + 1) * P], vec_t[:, 4 + c:5 + c], 0.0,
                                      ALU.add, ALU.max).then_inc(h2_ok, 1)
                dve.wait_ge(layer3, t + 1)
                dve.tensor_copy(y[:, t:t + 1], ps_h2[:, 2 * P:2 * P + 1]).then_inc(y_ok, 1)

            gram_out(0)
            gram_out(1)
            relu1(0)
            relu2(0)
            split_rows(2)
            relu1(1)
            gram_out(2)
            relu2(1)
            relu1(2)
            split_rows(3)
            gram_out(3)
            relu2(2)
            relu1(3)
            relu2(3)

        @block.tensor
        def _(pe):
            pe.wait_ge(ident_h_ok, 1)
            pe.wait_ge(ids_h_ok, 1)
            for t in range(TILES):
                last = pe.transpose(ps_ids[:, t * P:(t + 1) * P], ids_h[:, t, :], ident_h[:, :])
            last.then_inc(ids_turned, 1)
            pe.wait_ge(dense_in, 16)
            for t in range(TILES):
                last = pe.transpose(ps_dense[:, t, :], dense[:, t, :], ident[:, :])
            last.then_inc(dense_turned, 1)
            pe.wait_ge(vec_in, 48)
            pe.transpose(ps_vec, vec[:, :], ident[0:8, 0:8]).then_inc(vec_turned, 1)
            pe.wait_ge(ident_b_ok, 1)
            pe.wait_ge(id_rows_ok, 1)

            def turn(t):
                pe.wait_ge(emb3_ok, t + 1)
                for g in range(3):
                    n = 3 * t + g
                    if n >= 2:
                        pe.wait_ge(turned_copied, n - 1)
                    for k in range(8):
                        last = pe.transpose(ps_tr[n % 2][0:K3, k * P:(k + 1) * P], emb3[:, t % 2, 8 * g + k, :],
                                            ident_b[:, :])
                    last.then_inc(turned, 1)

            n = 0
            for q in range(PAIRS):
                for c, (q0, q1) in enumerate(SPLIT_CHUNKS):
                    if q == q0:
                        pe.wait_ge(tbl3_ok, c + 1)
                if q >= 2:
                    pe.wait_ge(look_copied, 2 * (q - 1))
                lo_n = LO[2 * q]
                for lo in range(lo_n):
                    for e in range(2):
                        pe.wait_ge(onehot_ok, n + 1)
                        last = pe.matmul(ps_look[q % 2][64 * e:64 * e + K3, :],
                                         lhsT=tbl3[:, LO_AT[2 * q + e] + lo, :], rhs=onehot[:, n % OH_RING, :],
                                         start=lo == 0, stop=lo == lo_n - 1)
                        last.then_inc(onehot_used, 1)
                        n += 1
                pe.wait_ge(onehot_used, n)
                pe.sem_inc(looked_up, 1)
                if q == 8:
                    turn(0)
            turn(1)

            def gram_tile(t):
                pe.wait_ge(small_ops[min(t, 1)], OPS_COUNT)
                pe.wait_ge(big_ops[t], OPS_COUNT)
                for k in range(FILLS):
                    m = FILLS * t + k
                    if m >= 2:
                        pe.wait_ge((gram_out_dve, gram_out_act)[k % 2], (m - 2) // 2 + 1)
                    for s in range(SPF):
                        b = SPF * k + s
                        last = pe.matmul(ps_gram[k % 2][0:FIELDS, s, 0:FIELDS], lhsT=lhs[:, t, :, b],
                                         rhs=rhs[:, t, :, b], start=True, stop=True)
                    last.then_inc(gram_ok, 1)

            def first(t):
                pe.wait_ge(z_in, Z_COUNT * (t + 1))
                pe.wait_ge(w1_in, 48)
                if t == 0:
                    pe.wait_ge(dense_t_ok, 1)
                else:
                    pe.wait_ge(h1_ok, 4 * t)
                for c in range(HIDDEN1 // P):
                    for s in range(SLOTS):
                        r = SLOT_ROWS[s]
                        last = pe.matmul(ps_h1[:, c, :], lhsT=w1[0:r, s, c * P:(c + 1) * P], rhs=z[0:r, s, :],
                                         start=s == 0, stop=s == SLOTS - 1)
                last.then_inc(layer1, 1)

            def second(t):
                pe.wait_ge(h1_ok, 4 * (t + 1))
                pe.wait_ge(w2_in, 16)
                if t == 0:
                    pe.wait_ge(vec_t_ok, 1)
                else:
                    pe.wait_ge(y_ok, t)
                for c in range(HIDDEN2 // P):
                    for k in range(HIDDEN1 // P):
                        last = pe.matmul(ps_h2[:, c * P:(c + 1) * P], lhsT=w2[:, k, c * P:(c + 1) * P],
                                         rhs=h1[:, k, :], start=k == 0, stop=k == HIDDEN1 // P - 1)
                last.then_inc(layer2, 1)
                pe.wait_ge(h2_ok, 2 * (t + 1))
                for c in range(HIDDEN2 // P):
                    last = pe.matmul(ps_h2[:, 2 * P:2 * P + 1], lhsT=h2[:, c, :], rhs=vec_t[:, 6 + c:7 + c],
                                     start=c == 0, stop=c == HIDDEN2 // P - 1)
                last.then_inc(layer3, 1)

            gram_tile(0)
            gram_tile(1)
            first(0)
            second(0)
            turn(2)
            first(1)
            gram_tile(2)
            second(1)
            first(2)
            turn(3)
            gram_tile(3)
            second(2)
            first(3)
            second(3)


def slot_rows():
    def pair(i, j):
        x, y = sorted((ORDER[i], ORDER[j]))
        return x * FIELDS - x * (x + 1) // 2 + y - x - 1

    where = []
    for j in range(FIELDS):
        for i in range(j):
            g = j // G12
            if j >= 48:
                at = (DENSE_SLOT, FINAL_AT) if i == 48 else (2 * (i // 12) + j - 48, LAST_AT + i % 12)
            elif i < G12 * g:
                at = (j - G12 * g, RECT_AT[g] + i)
            else:
                at = (j - G12 * g - 1, TRI_AT + 11 * g + i - G12 * g)
            where.append((*at, pair(i, j)))
    where += [(DENSE_SLOT, DENSE_AT + d, FIELDS * (FIELDS - 1) // 2 + d) for d in range(DIM)]
    return where


_INS = ["dense_ctx", "ids"] + [f"tbl_{f}" for f in range(FIELDS)] + ["w1_slots", "b_top1", "W_top2", "b_top2", "W_top3"]


def kernel(**inputs):
    import numpy as _np
    import concourse.bacc as _bacc
    from concourse import mybir as _mybir
    from concourse.bass_utils import run_bass_kernel_spmd as _run

    given = {name: _np.asarray(x) for name, x in inputs.items()}
    given["ids"] = given["ids"][:, ORDER]
    w1 = given["W_top1"]
    slots = _np.zeros((P, SLOTS, HIDDEN1), w1.dtype)
    where = _np.array(slot_rows())
    slots[where[:, 1], where[:, 0]] = w1[where[:, 2]]
    given["w1_slots"] = slots

    nc = _bacc.Bacc("TRN2", target_bir_lowering=False, num_devices=1)
    arrays, aps = {}, {}
    for name in _INS:
        x = _np.ascontiguousarray(given[name])
        arrays[f"in_{name}"] = x
        aps[name] = nc.dram_tensor(f"in_{name}", x.shape, _mybir.dt.from_np(x.dtype), kind="ExternalInput").ap()
    out = nc.dram_tensor("out_0", (BATCH, 1), _mybir.dt.float32, kind="ExternalOutput").ap()
    dlrm_tower(nc, aps, out)
    r = _run(nc, [arrays], core_ids=[0])
    return r.results[0]["out_0"]
```

```python
import concourse.bass as bass
from concourse import mybir
from contextlib import ExitStack

BATCH = 512
FIELDS = 50
DIM = 16
P = 128
TILES = BATCH // P
HIDDEN1, HIDDEN2 = 512, 256
ROWS = [1250, 1000, 125000, 125000, 1250, 1000, 1250, 1000, 125000, 1000, 12500, 1250, 125000, 125000, 12500,
        1000, 125000, 1000, 12500, 125000, 1000, 1250, 125000, 1250, 1250, 125000, 1000, 12500, 1250, 12500,
        125000, 1000, 12500, 12500, 12500, 1000, 125000, 125000, 125000, 12500, 1250, 12500, 1250, 1250, 12500,
        1250, 1250, 1250, 1000, 1000]

HI = 125
SMALL = [f for f in range(FIELDS) if ROWS[f] == 1250] + [f for f in range(FIELDS) if ROWS[f] == 1000]
BIG = [f for f in range(FIELDS) if ROWS[f] > 1250]
ORDER = SMALL + BIG
NS, NB = len(SMALL), len(BIG)
GROUPS = [(0, 4), (4, 8), (8, 12), (12, 14), (14, 18), (18, 22), (22, 26)]
LO = [ROWS[f] // HI for f in SMALL]
LO_AT = [sum(LO[:s]) for s in range(NS + 1)]
LOOKS = [sum(LO[g[0]] for g in GROUPS[:n]) for n in range(len(GROUPS) + 1)]
BLOCKS = 7
MID_B, HIGH_B, LOW_B = 0, 1, 2
K3 = 3 * DIM
KG = 6 * DIM

G12 = 12
SLOTS = 12
RECT_AT = {1: 0, 2: 12, 3: 36}
TRI_AT = 72
LAST_AT = 116
DENSE_AT, DENSE_SLOT = 72, 11
FINAL_AT = 88
SLOT_ROWS = [128] * 8 + [116] * 3 + [FINAL_AT + 1]

SPF = 8
FILLS = P // SPF
BANKS = 4
DVE_FILLS = [k for k in range(FILLS) if k % 2 == 0]
ACT_FILLS = [k for k in range(FILLS) if k % 2 == 1]
OH_RING = 3
ID_RING = 2
TURN = 8
ROUNDS = NB // TURN


def dlrm_tower(nc, a, out):
    f32, bf16, fp16, i32 = mybir.dt.float32, mybir.dt.bfloat16, mybir.dt.float16, mybir.dt.int32
    ALU = mybir.AluOpType
    ACT = mybir.ActivationFunctionType
    ctx = ExitStack()
    with ctx:
        def sb(name, shape, dt):
            return ctx.enter_context(nc.sbuf_tensor(name, shape, dt))

        def pb(name, shape, dt):
            return ctx.enter_context(nc.psum_tensor(name, shape, dt))

        def sem(name):
            return ctx.enter_context(nc.semaphore(name))

        id_scratch = nc.dram_tensor("id_scratch", (NS, BATCH), fp16, kind="Internal").ap()

        ids = sb("ids", [P, TILES, FIELDS], i32)
        ids_h = sb("ids_h", [P, TILES, NS], fp16)
        id_rows = sb("id_rows", [NS, BATCH], fp16)
        id_all = sb("id_all", [HI, ID_RING, 4, BATCH], fp16)
        iota_i = sb("iota_i", [HI, 18], i32)
        iota_f = sb("iota_f", [HI, 18], f32)
        ident = sb("ident", [P, P], f32)
        ident_b = sb("ident_b", [P, P], bf16)
        ident_h = sb("ident_h", [P, P], fp16)
        gram_mem = sb("gram_mem", [P, FIELDS * P], f32)
        gram = gram_mem[0:FIELDS, :].rearrange("i (j b) -> i j b", b=P)
        tbl = gram_mem[0:HI, 0:LO_AT[NS] * DIM].rearrange("p (l d) -> p l d", d=DIM)
        w1 = sb("w1", [P, SLOTS, HIDDEN1], f32)
        tbl3 = w1[0:HI, :, :].rearrange("p s n -> p (s n)")[:, 0:LO_AT[NS] * K3 // 2].bitcast(bf16)
        tbl3 = tbl3.rearrange("p (l k) -> p l k", k=K3)
        onehot = sb("onehot", [HI, OH_RING, 4, BATCH], bf16)
        emb = sb("emb", [P, 2, NB, DIM], f32)
        emb3 = sb("emb3", [P, 2, NB, BLOCKS, DIM], bf16)
        lhs = sb("lhs", [KG, TILES, FIELDS, P], bf16)
        rhs = sb("rhs", [KG, TILES, FIELDS, P], bf16)
        z = sb("z", [P, 2, SLOTS, P], f32)
        dense = sb("dense", [P, TILES, DIM], f32)
        dense_t = sb("dense_t", [DIM, BATCH], f32)
        w2 = sb("w2", [P, HIDDEN1 // P, HIDDEN2], f32)
        vec = sb("vec", [8, P], f32)
        vec_t = sb("vec_t", [P, 8], f32)
        h1 = sb("h1", [P, HIDDEN1 // P, P], f32)
        h2 = sb("h2", [P, HIDDEN2 // P, P], f32)
        y = sb("y", [P, TILES], f32)

        bank = [pb(f"bank{i}", [P, 512], f32) for i in range(BANKS)]
        ps_tr = [pb(f"ps_tr{i}", [P, TURN, P], bf16) for i in range(2)]
        ps_h1 = pb("ps_h1", [P, HIDDEN1 // P, P], f32)
        ps_h2 = pb("ps_h2", [P, 512], f32)
        ps_ids = ps_tr[0][0:NS, 0:TILES, :].bitcast(fp16)
        ps_dense = ps_h1[0:DIM, :, :]
        ps_vec = ps_h2[:, 0:8]

        ids_in = sem("ids_in")
        tbl_in = [sem(f"tbl_in{c}") for c in range(len(GROUPS))]
        w1_in, w2_in, vec_in, dense_in = sem("w1_in"), sem("w2_in"), sem("vec_in"), sem("dense_in")
        ident_zero, ident_ok, ident_b_ok = sem("ident_zero"), sem("ident_ok"), sem("ident_b_ok")
        ident_h_ok = sem("ident_h_ok")
        iota_ok, iota_f_ok = sem("iota_ok"), sem("iota_f_ok")
        ids_h_ok, ids_turned, id_rows_ok = sem("ids_h_ok"), sem("ids_turned"), sem("id_rows_ok")
        id_scratch_ok = sem("id_scratch_ok")
        id_all_in = [sem(f"id_all_in{i}") for i in range(ID_RING)]
        high_ok, rest_ok, mid_ok, tbl3_ok = sem("high_ok"), sem("rest_ok"), sem("mid_ok"), sem("tbl3_ok")
        onehot_ok, onehot_used = sem("onehot_ok"), sem("onehot_used")
        look_copied = sem("look_copied")
        rows_in = [sem(f"rows_in{t}") for t in range(TILES)]
        e_high, e_rest, e_mid, emb3_ok = sem("e_high"), sem("e_rest"), sem("e_mid"), sem("emb3_ok")
        turned, left_ok, right_ok = sem("turned"), sem("left_ok"), sem("right_ok")
        left_in = [sem(f"left_in{i}") for i in range(2)]
        right_in = [sem(f"right_in{i}") for i in range(2)]
        gram_ok = sem("gram_ok")
        gram_out_act, gram_out_dve = sem("gram_out_act"), sem("gram_out_dve")
        z_in = [sem(f"z_in{t}") for t in range(TILES)]
        z_in_pool = sem("z_in_pool")
        dense_z = [sem(f"dense_z{t}") for t in range(TILES)]
        dense_turned, dense_t_ok, vec_turned, vec_t_ok = (sem("dense_turned"), sem("dense_t_ok"),
                                                          sem("vec_turned"), sem("vec_t_ok"))
        layer1, h1_ok, layer2, h2_ok = sem("layer1"), sem("h1_ok"), sem("layer2"), sem("h2_ok")
        layer3, y_ok, out_ok = sem("layer3"), sem("y_ok"), sem("out_ok")

        moves = [(RECT_AT[g], 12 * g, 0, 12, 0, 12 * g) for g in (1, 2, 3)]
        moves += [(TRI_AT + 11 * g, 11, 0, 11, 12 * g, 12 * g + 1) for g in range(4)]
        moves += [(LAST_AT, 12, 2 * q, 2, 12 * q, 48) for q in range(4)]
        moves += [(FINAL_AT, 1, DENSE_SLOT, 1, 48, 49)]
        POOL_MOVES = 4
        Z_COUNT = 16 * len(moves)

        def move(eng, done, t, row, rows, slot, slots, i, j):
            eng.dma_start(z[row:row + rows, t % 2, slot:slot + slots, :],
                          gram[i:i + rows, j:j + slots, :]).then_inc(done, 16)

        left_copies = [(3 * DIM, HIGH_B * DIM, DIM), (4 * DIM, HIGH_B * DIM, DIM), (5 * DIM, MID_B * DIM, DIM)]
        right_copies = [(0, DIM, 5 * DIM), (5 * DIM, MID_B * DIM, DIM)]

        def load_tables(eng, g):
            for s in range(*GROUPS[g]):
                eng.dma_start(tbl[:, LO_AT[s]:LO_AT[s + 1], :],
                              a[f"tbl_{SMALL[s]}"].rearrange("(p l) d -> p l d", l=LO[s])).then_inc(tbl_in[g], 16)

        def table_rows(g):
            return slice(LO_AT[GROUPS[g][0]], LO_AT[GROUPS[g][1]])

        block = ctx.enter_context(nc.Block())

        @block.sync
        def _(sp):
            sp.dma_start(ids[:, :, :], a["ids"].rearrange("(p t) f -> p t f", t=TILES)).then_inc(ids_in, 16)
            sp.wait_ge(id_rows_ok, 1)
            sp.dma_start(id_scratch, id_rows[:, :]).then_inc(id_scratch_ok, 16)
            load_tables(sp, 2)
            sp.wait_ge(id_scratch_ok, 16)

            def spread_ids(g):
                if g >= ID_RING:
                    sp.wait_ge(onehot_ok, LOOKS[g - ID_RING + 1])
                s0, s1 = GROUPS[g]
                sp.dma_start(id_all[:, g % ID_RING, 0:s1 - s0, :],
                             id_scratch[s0:s1, :].rearrange("(o f) b -> o f b", o=1).broadcast_to((HI, s1 - s0, BATCH))
                             ).then_inc(id_all_in[g % ID_RING], 16)

            spread_ids(0)
            spread_ids(1)
            load_tables(sp, 3)
            load_tables(sp, 4)
            load_tables(sp, 5)
            load_tables(sp, 6)
            sp.dma_start(vec[0:4, :], a["b_top1"].rearrange("(c p) -> c p", p=P)).then_inc(vec_in, 16)
            sp.dma_start(vec[4:6, :], a["b_top2"].rearrange("(c p) -> c p", p=P)).then_inc(vec_in, 16)
            sp.dma_start(vec[6:8, :], a["W_top3"].rearrange("(c p) n -> c (p n)", p=P)).then_inc(vec_in, 16)
            sp.dma_start(dense[:, :, :], a["dense_ctx"].rearrange("(p t) d -> p t d", t=TILES)).then_inc(dense_in, 16)
            for g in range(2, len(GROUPS)):
                spread_ids(g)
            sp.dma_start(w2[:, :, :], a["W_top2"].rearrange("(c p) n -> p c n", p=P)).then_inc(w2_in, 16)

            def dense_to_z(t):
                sp.dma_start(z[DENSE_AT:DENSE_AT + DIM, t % 2, DENSE_SLOT, :],
                             dense_t[:, t * P:(t + 1) * P]).then_inc(dense_z[t], 16)

            def spread_parts(n, tiles):
                for row, src, rows in left_copies:
                    sp.dma_start(lhs[row:row + rows, tiles, 0:NS, :],
                                 lhs[src:src + rows, tiles, 0:NS, :]).then_inc(left_in[n], 16)
                sp.wait_ge(left_in[n], 16 * len(left_copies))
                for row, src, rows in right_copies:
                    sp.dma_start(rhs[row:row + rows, tiles, 0:NS, :],
                                 lhs[src:src + rows, tiles, 0:NS, :]).then_inc(right_in[n], 16)

            sp.wait_ge(dense_t_ok, 1)
            dense_to_z(0)
            dense_to_z(1)
            sp.wait_ge(look_copied, NS)
            spread_parts(0, slice(0, 1))
            sp.wait_ge(onehot_used, LOOKS[-1])
            for s in range(0, SLOTS, 4):
                sp.dma_start(w1[:, s:s + 4, :], a["w1_slots"][:, s:s + 4, :]).then_inc(w1_in, 16)
            spread_parts(1, slice(1, TILES))

            for t in range(TILES):
                if t >= 2:
                    sp.wait_ge(layer1, t - 1)
                    dense_to_z(t)
                sp.wait_ge(gram_out_act, len(ACT_FILLS) * (t + 1))
                sp.wait_ge(gram_out_dve, len(DVE_FILLS) * (t + 1))
                for m in (moves if t < TILES - 1 else moves[POOL_MOVES:]):
                    move(sp, z_in[t], t, *m)
            sp.wait_ge(y_ok, TILES)
            sp.dma_start(out.rearrange("(p t) o -> p (t o)", t=TILES), y[:, :]).then_inc(out_ok, 16)
            sp.wait_ge(out_ok, 16)

        @block.gpsimd
        def _(pool):
            pool.memset(ident[:, :], 0.0).then_inc(ident_zero, 1)
            pool.iota(iota_i[:, 0:10], pattern=[[1, 10]], base=0, channel_multiplier=10)
            pool.iota(iota_i[:, 10:18], pattern=[[1, 8]], base=0, channel_multiplier=8).then_inc(iota_ok, 1)
            pool.wait_ge(ident_zero, 1)
            pool.affine_select(out=ident[:, :], in_=ident[:, :], compare_op=ALU.not_equal, fill=1.0, base=0,
                               pattern=[[-1, P]], channel_multiplier=1).then_inc(ident_ok, 1)
            pool.wait_ge(ids_in, 16)
            for t in range(TILES):
                if t >= 2:
                    pool.wait_ge(emb3_ok, t - 1)
                for k, f in enumerate(BIG):
                    pool.indirect_dma_start(
                        out=emb[:, t % 2, k, :], out_offset=None, in_=a[f"tbl_{f}"],
                        in_offset=bass.IndirectOffsetOnAxis(ap=ids[:, t, NS + k:NS + k + 1], axis=0),
                    ).then_inc(rows_in[t], 16)
            pool.wait_ge(layer1, TILES - 2)
            pool.wait_ge(gram_out_act, len(ACT_FILLS) * TILES)
            pool.wait_ge(gram_out_dve, len(DVE_FILLS) * TILES)
            for m in moves[:POOL_MOVES]:
                move(pool, z_in_pool, TILES - 1, *m)

        @block.scalar
        def _(act):
            load_tables(act, 0)
            load_tables(act, 1)

            def high_part(g):
                act.wait_ge(tbl_in[g], 16 * (GROUPS[g][1] - GROUPS[g][0]))
                act.activation(tbl3[:, table_rows(g), HIGH_B * DIM:(HIGH_B + 1) * DIM], tbl[:, table_rows(g), :],
                               ACT.Copy).then_inc(high_ok, 1)

            def middle_part(g):
                act.wait_ge(rest_ok, g + 1)
                act.activation(tbl3[:, table_rows(g), MID_B * DIM:(MID_B + 1) * DIM], tbl[:, table_rows(g), :],
                               ACT.Copy).then_inc(mid_ok, 1)

            def copy_looked(g):
                act.wait_ge(onehot_used, LOOKS[g + 1])
                for s in range(*GROUPS[g]):
                    e = s - GROUPS[g][0]
                    act.activation(lhs[0:K3, :, s, :],
                                   bank[2 * (g % 2) + e // 2][64 * (e % 2):64 * (e % 2) + K3, :]
                                   .rearrange("k (t p) -> k t p", p=P), ACT.Copy).then_inc(look_copied, 1)

            def copy_turned(side, t, r, done):
                act.wait_ge(turned, ROUNDS * t + r + 1)
                act.activation((lhs, rhs)[side][:, t, NS + TURN * r:NS + TURN * (r + 1), :],
                               ps_tr[side][0:KG, :, :], ACT.Copy).then_inc(done, 1)

            def gram_out(t):
                if t >= 1:
                    act.wait_ge(z_in[t - 1], Z_COUNT)
                for k in ACT_FILLS:
                    act.wait_ge(gram_ok, FILLS * t + k + 1)
                    act.activation(gram[:, :, SPF * k:SPF * k + SPF],
                                   bank[k % BANKS][0:FIELDS, 0:SPF * FIELDS].rearrange("i (b j) -> i j b", b=SPF),
                                   ACT.Copy).then_inc(gram_out_act, 1)

            high_part(0)
            middle_part(0)
            high_part(1)
            for g in range(len(GROUPS)):
                if g >= 1:
                    copy_looked(g - 1)
                if g >= 5:
                    copy_turned(0, 0, g - 5, left_ok)
                    copy_turned(1, 0, g - 5, right_ok)
                if g + 1 < len(GROUPS):
                    middle_part(g + 1)
                if g + 2 < len(GROUPS):
                    high_part(g + 2)
            copy_looked(len(GROUPS) - 1)
            copy_turned(0, 0, 2, left_ok)
            copy_turned(1, 0, 2, right_ok)
            for r in range(ROUNDS):
                copy_turned(0, 1, r, left_ok)
            gram_out(0)
            gram_out(1)
            for t in range(2, TILES):
                for r in range(ROUNDS):
                    copy_turned(0, t, r, left_ok)
                gram_out(t)

        @block.vector
        def _(dve):
            dve.wait_ge(ident_ok, 1)
            dve.tensor_copy(ident_h[:, :], ident[:, :]).then_inc(ident_h_ok, 1)
            dve.wait_ge(ids_in, 16)
            dve.tensor_copy(ids_h[:, :, :], ids[:, :, 0:NS]).then_inc(ids_h_ok, 1)
            dve.tensor_copy(ident_b[:, :], ident[:, :]).then_inc(ident_b_ok, 1)
            dve.wait_ge(iota_ok, 1)
            dve.tensor_copy(iota_f[:, :], iota_i[:, :]).then_inc(iota_f_ok, 1)
            dve.wait_ge(ids_turned, 1)
            dve.tensor_copy(id_rows[:, :].rearrange("f (t p) -> f t p", p=P), ps_ids).then_inc(id_rows_ok, 1)

            def copy_dense_vec():
                dve.wait_ge(dense_turned, 1)
                dve.tensor_copy(dense_t[:, :].rearrange("d (t p) -> d t p", p=P), ps_dense).then_inc(dense_t_ok, 1)
                dve.wait_ge(vec_turned, 1)
                dve.tensor_copy(vec_t[:, :], ps_vec).then_inc(vec_t_ok, 1)

            def rest(g):
                dve.wait_ge(high_ok, g + 1)
                dve.tensor_tensor(tbl[:, table_rows(g), :], tbl[:, table_rows(g), :],
                                  tbl3[:, table_rows(g), HIGH_B * DIM:(HIGH_B + 1) * DIM],
                                  ALU.subtract).then_inc(rest_ok, 1)

            def low_part(g):
                dve.wait_ge(mid_ok, g + 1)
                dve.tensor_tensor(tbl3[:, table_rows(g), LOW_B * DIM:(LOW_B + 1) * DIM], tbl[:, table_rows(g), :],
                                  tbl3[:, table_rows(g), MID_B * DIM:(MID_B + 1) * DIM],
                                  ALU.subtract).then_inc(tbl3_ok, 1)

            def split_rows(t):
                e, e3 = emb[:, t % 2, :, :], emb3[:, t % 2, :, :, :]
                twice = e.rearrange("p f (o d) -> p f o d", o=1).broadcast_to((P, NB, 2, DIM))
                dve.wait_ge(rows_in[t], 16 * NB)
                if t >= 2:
                    dve.wait_ge(turned, ROUNDS * (t - 1))
                dve.tensor_copy(e3[:, :, 3:5, :], twice).then_inc(e_high, 1)
                dve.wait_ge(e_high, t + 1)
                dve.tensor_copy(e3[:, :, HIGH_B, :], e3[:, :, 3, :])
                dve.tensor_tensor(e, e, e3[:, :, 3, :], ALU.subtract).then_inc(e_rest, 1)
                dve.wait_ge(e_rest, t + 1)
                dve.tensor_copy(e3[:, :, 5:7, :], twice).then_inc(e_mid, 1)
                dve.wait_ge(e_mid, t + 1)
                dve.tensor_copy(e3[:, :, MID_B, :], e3[:, :, 5, :])
                dve.tensor_tensor(e3[:, :, LOW_B, :], e, e3[:, :, 5, :], ALU.subtract).then_inc(emb3_ok, 1)

            def copy_turned(t):
                for r in range(ROUNDS):
                    dve.wait_ge(turned, ROUNDS * t + r + 1)
                    dve.tensor_copy(rhs[:, t, NS + TURN * r:NS + TURN * (r + 1), :],
                                    ps_tr[1][0:KG, :, :]).then_inc(right_ok, 1)

            dve.wait_ge(iota_f_ok, 1)
            rest(0)
            low_part(0)
            for g, (s0, s1) in enumerate(GROUPS):
                dve.wait_ge(id_all_in[g % ID_RING], 16 * (g // ID_RING + 1))
                base = 0 if LO[s0] == 10 else 10
                for lo in range(LO[s0]):
                    n = LOOKS[g] + lo
                    if n >= OH_RING:
                        dve.wait_ge(onehot_used, n - OH_RING + 1)
                    dve.tensor_scalar(onehot[:, n % OH_RING, 0:s1 - s0, :], id_all[:, g % ID_RING, 0:s1 - s0, :],
                                      iota_f[:, base + lo:base + lo + 1], None, ALU.is_equal).then_inc(onehot_ok, 1)
                    if lo == 3 and g + 1 < len(GROUPS):
                        rest(g + 1)
                if g + 1 < len(GROUPS):
                    low_part(g + 1)
                if g == 2:
                    copy_dense_vec()
                if g == 3:
                    split_rows(0)
            split_rows(1)
            copy_turned(1)

            def gram_out(t):
                if t >= 1:
                    dve.wait_ge(z_in[t - 1], Z_COUNT)
                for k in DVE_FILLS:
                    dve.wait_ge(gram_ok, FILLS * t + k + 1)
                    dve.tensor_copy(gram[:, :, SPF * k:SPF * k + SPF],
                                    bank[k % BANKS][0:FIELDS, 0:SPF * FIELDS].rearrange("i (b j) -> i j b", b=SPF)
                                    ).then_inc(gram_out_dve, 1)

            def relu1(t):
                dve.wait_ge(layer1, t + 1)
                if t >= 1:
                    dve.wait_ge(layer2, t)
                for c in range(HIDDEN1 // P):
                    dve.tensor_scalar(h1[:, c, :], ps_h1[:, c, :], vec_t[:, c:c + 1], 0.0, ALU.add, ALU.max
                                      ).then_inc(h1_ok, 1)

            def relu2(t):
                dve.wait_ge(layer2, t + 1)
                if t >= 1:
                    dve.wait_ge(layer3, t)
                for c in range(HIDDEN2 // P):
                    dve.tensor_scalar(h2[:, c, :], ps_h2[:, c * P:(c + 1) * P], vec_t[:, 4 + c:5 + c], 0.0,
                                      ALU.add, ALU.max).then_inc(h2_ok, 1)
                dve.wait_ge(layer3, t + 1)
                dve.tensor_copy(y[:, t:t + 1], ps_h2[:, 2 * P:2 * P + 1]).then_inc(y_ok, 1)

            gram_out(0)
            gram_out(1)
            relu1(0)
            split_rows(2)
            copy_turned(2)
            gram_out(2)
            relu2(0)
            relu1(1)
            relu2(1)
            split_rows(3)
            copy_turned(3)
            gram_out(3)
            relu1(2)
            relu2(2)
            relu1(3)
            relu2(3)

        @block.tensor
        def _(pe):
            pe.wait_ge(ident_h_ok, 1)
            pe.wait_ge(ids_h_ok, 1)
            for t in range(TILES):
                last = pe.transpose(ps_ids[:, t, :], ids_h[:, t, :], ident_h[:, :])
            last.then_inc(ids_turned, 1)
            pe.wait_ge(ident_b_ok, 1)
            pe.wait_ge(id_rows_ok, 1)

            def turn_dense_vec():
                pe.wait_ge(dense_in, 16)
                for t in range(TILES):
                    last = pe.transpose(ps_dense[:, t, :], dense[:, t, :], ident[:, :])
                last.then_inc(dense_turned, 1)
                pe.wait_ge(vec_in, 48)
                pe.transpose(ps_vec, vec[:, :], ident[0:8, 0:8]).then_inc(vec_turned, 1)

            def turn(t, r):
                pe.wait_ge(emb3_ok, t + 1)
                n = ROUNDS * t + r
                if n >= 1:
                    pe.wait_ge(left_ok, n)
                    pe.wait_ge(right_ok, n)
                e3 = emb3[:, t % 2, :, :, :].rearrange("p f k d -> p f (k d)")
                for side in range(2):
                    for k in range(TURN):
                        last = pe.transpose(ps_tr[side][0:KG, k, :],
                                            e3[:, TURN * r + k, DIM * side:DIM * side + KG], ident_b[:, :])
                last.then_inc(turned, 1)

            for g, (s0, s1) in enumerate(GROUPS):
                pe.wait_ge(tbl3_ok, g + 1)
                if g >= 2:
                    pe.wait_ge(look_copied, GROUPS[g - 2][1])
                for lo in range(LO[s0]):
                    n = LOOKS[g] + lo
                    pe.wait_ge(onehot_ok, n + 1)
                    for e in range(s1 - s0):
                        at = 64 * (e % 2)
                        last = pe.matmul(bank[2 * (g % 2) + e // 2][at:at + K3, :],
                                         lhsT=tbl3[:, LO_AT[s0 + e] + lo, :], rhs=onehot[:, n % OH_RING, e, :],
                                         start=lo == 0, stop=lo == LO[s0] - 1)
                    last.then_inc(onehot_used, 1)
                if g == 1:
                    turn_dense_vec()
                if g >= 4:
                    turn(0, g - 4)
            for r in range(ROUNDS):
                turn(1, r)

            def gram_tile(t):
                pe.wait_ge(right_in[min(t, 1)], 16 * len(right_copies))
                pe.wait_ge(left_ok, ROUNDS * (t + 1))
                pe.wait_ge(right_ok, ROUNDS * (t + 1))
                if t == 0:
                    pe.wait_ge(look_copied, NS)
                for k in range(FILLS):
                    before = FILLS * t + k - BANKS
                    if before >= 0:
                        k0 = before % FILLS
                        if k0 in DVE_FILLS:
                            pe.wait_ge(gram_out_dve, len(DVE_FILLS) * (before // FILLS) + DVE_FILLS.index(k0) + 1)
                        else:
                            pe.wait_ge(gram_out_act, len(ACT_FILLS) * (before // FILLS) + ACT_FILLS.index(k0) + 1)
                    for s in range(SPF):
                        b = SPF * k + s
                        last = pe.matmul(bank[k % BANKS][0:FIELDS, s * FIELDS:(s + 1) * FIELDS], lhsT=lhs[:, t, :, b],
                                         rhs=rhs[:, t, :, b], start=True, stop=True)
                    last.then_inc(gram_ok, 1)

            def first(t, chunks):
                pe.wait_ge(z_in[t], Z_COUNT if t < TILES - 1 else Z_COUNT - 16 * POOL_MOVES)
                if t == TILES - 1:
                    pe.wait_ge(z_in_pool, 16 * POOL_MOVES)
                pe.wait_ge(dense_z[t], 16)
                pe.wait_ge(w1_in, 48)
                if t == 0:
                    pe.wait_ge(dense_t_ok, 1)
                else:
                    pe.wait_ge(h1_ok, 4 * t)
                for c in chunks:
                    for s in range(SLOTS):
                        r = SLOT_ROWS[s]
                        last = pe.matmul(ps_h1[:, c, :], lhsT=w1[0:r, s, c * P:(c + 1) * P], rhs=z[0:r, t % 2, s, :],
                                         start=s == 0, stop=s == SLOTS - 1)
                if c == HIDDEN1 // P - 1:
                    last.then_inc(layer1, 1)

            def second(t):
                pe.wait_ge(h1_ok, 4 * (t + 1))
                pe.wait_ge(w2_in, 16)
                if t == 0:
                    pe.wait_ge(vec_t_ok, 1)
                else:
                    pe.wait_ge(y_ok, t)
                for c in range(HIDDEN2 // P):
                    for k in range(HIDDEN1 // P):
                        last = pe.matmul(ps_h2[:, c * P:(c + 1) * P], lhsT=w2[:, k, c * P:(c + 1) * P],
                                         rhs=h1[:, k, :], start=k == 0, stop=k == HIDDEN1 // P - 1)
                last.then_inc(layer2, 1)
                pe.wait_ge(h2_ok, 2 * (t + 1))
                for c in range(HIDDEN2 // P):
                    last = pe.matmul(ps_h2[:, 2 * P:2 * P + 1], lhsT=h2[:, c, :], rhs=vec_t[:, 6 + c:7 + c],
                                     start=c == 0, stop=c == HIDDEN2 // P - 1)
                last.then_inc(layer3, 1)

            every, front, back = range(4), range(2), range(2, 4)
            gram_tile(0)
            gram_tile(1)
            first(0, every)
            for r in range(ROUNDS):
                turn(2, r)
            first(1, front)
            gram_tile(2)
            second(0)
            first(1, back)
            second(1)
            first(2, front)
            for r in range(ROUNDS):
                turn(3, r)
            gram_tile(3)
            first(2, back)
            second(2)
            first(3, every)
            second(3)


def slot_rows():
    def pair(i, j):
        x, y = sorted((ORDER[i], ORDER[j]))
        return x * FIELDS - x * (x + 1) // 2 + y - x - 1

    where = []
    for j in range(FIELDS):
        for i in range(j):
            g = j // G12
            if j >= 48:
                at = (DENSE_SLOT, FINAL_AT) if i == 48 else (2 * (i // 12) + j - 48, LAST_AT + i % 12)
            elif i < G12 * g:
                at = (j - G12 * g, RECT_AT[g] + i)
            else:
                at = (j - G12 * g - 1, TRI_AT + 11 * g + i - G12 * g)
            where.append((*at, pair(i, j)))
    where += [(DENSE_SLOT, DENSE_AT + d, FIELDS * (FIELDS - 1) // 2 + d) for d in range(DIM)]
    return where


_INS = ["dense_ctx", "ids"] + [f"tbl_{f}" for f in range(FIELDS)] + ["w1_slots", "b_top1", "W_top2", "b_top2", "W_top3"]


def kernel(**inputs):
    import numpy as _np
    import concourse.bacc as _bacc
    from concourse import mybir as _mybir
    from concourse.bass_utils import run_bass_kernel_spmd as _run

    given = {name: _np.asarray(x) for name, x in inputs.items()}
    given["ids"] = given["ids"][:, ORDER]
    w1 = given["W_top1"]
    slots = _np.zeros((P, SLOTS, HIDDEN1), w1.dtype)
    where = _np.array(slot_rows())
    slots[where[:, 1], where[:, 0]] = w1[where[:, 2]]
    given["w1_slots"] = slots

    nc = _bacc.Bacc("TRN2", target_bir_lowering=False, num_devices=1)
    arrays, aps = {}, {}
    for name in _INS:
        x = _np.ascontiguousarray(given[name])
        arrays[f"in_{name}"] = x
        aps[name] = nc.dram_tensor(f"in_{name}", x.shape, _mybir.dt.from_np(x.dtype), kind="ExternalInput").ap()
    out = nc.dram_tensor("out_0", (BATCH, 1), _mybir.dt.float32, kind="ExternalOutput").ap()
    dlrm_tower(nc, aps, out)
    r = _run(nc, [arrays], core_ids=[0])
    return r.results[0]["out_0"]
```

```python
import concourse.bass as bass
from concourse import mybir
from contextlib import ExitStack

BATCH = 512
FIELDS = 50
DIM = 16
P = 128
TILES = BATCH // P
HIDDEN1, HIDDEN2 = 512, 256
ROWS = [1250, 1000, 125000, 125000, 1250, 1000, 1250, 1000, 125000, 1000, 12500, 1250, 125000, 125000, 12500,
        1000, 125000, 1000, 12500, 125000, 1000, 1250, 125000, 1250, 1250, 125000, 1000, 12500, 1250, 12500,
        125000, 1000, 12500, 12500, 12500, 1000, 125000, 125000, 125000, 12500, 1250, 12500, 1250, 1250, 12500,
        1250, 1250, 1250, 1000, 1000]

HI = 125
SMALL = [f for f in range(FIELDS) if ROWS[f] == 1250] + [f for f in range(FIELDS) if ROWS[f] == 1000]
BIG = [f for f in range(FIELDS) if ROWS[f] > 1250]
ORDER = SMALL + BIG
NS, NB = len(SMALL), len(BIG)
GROUPS = [(0, 6), (6, 14), (14, 20), (20, 26)]
GROUP = 8
PIECES = [(0, 3), (3, 6)] + GROUPS[1:]
LO = [ROWS[f] // HI for f in SMALL]
LO_AT = [sum(LO[:s]) for s in range(NS + 1)]
HALF = BATCH // 2
STEPS = 2 * len(GROUPS)
SPREADS = [(3, 0, 0, GROUPS[3][0]), (4, 0, *GROUPS[3]), (8, 1, 0, NS)]
LOOKS = [0]
for _n in range(STEPS):
    LOOKS.append(LOOKS[-1] + LO[GROUPS[_n % len(GROUPS)][0]])
BLOCKS = 7
MID_B, HIGH_B, LOW_B = 0, 1, 2
K3 = 3 * DIM
KG = 6 * DIM

SLOTS = 11
MOVES = [(0, 11, 0, 11, 0, 11), (11, 22, 0, 11, 0, 22), (33, 33, 0, 11, 0, 33), (66, 44, 0, 6, 0, 44),
         (110, 10, 0, 10, 0, 1),
         (66, 10, 6, 5, 11, 17), (76, 5, 6, 5, 11, 12),
         (81, 10, 6, 5, 33, 39), (91, 5, 6, 5, 33, 34),
         (96, 14, 6, 5, 22, 28), (120, 5, 0, 5, 22, 23),
         (120, 5, 5, 5, 44, 45)]
DENSE_AT, DENSE_SLOT = 110, 10
SLOT_ROWS = [125] * 10 + [126]

SPF = 512 // FIELDS
FILLS = -(-P // SPF)
GRAM_BANKS = 5
DVE_FILLS = list(range(1, FILLS, 2))
ACT_FILLS = [k for k in range(FILLS) if k not in DVE_FILLS]
GROUPS_CUT = 2
PARTS_CUT = LO_AT[GROUPS[GROUPS_CUT][0]]
OH_RING = 3
ID_RING = 2
TURN = 8
ROUNDS = NB // TURN


def dlrm_tower(nc, a, out):
    f32, bf16, fp16, i32 = mybir.dt.float32, mybir.dt.bfloat16, mybir.dt.float16, mybir.dt.int32
    ALU = mybir.AluOpType
    ACT = mybir.ActivationFunctionType
    ctx = ExitStack()
    with ctx:
        def sb(name, shape, dt):
            return ctx.enter_context(nc.sbuf_tensor(name, shape, dt))

        def pb(name, shape, dt):
            return ctx.enter_context(nc.psum_tensor(name, shape, dt))

        def sem(name):
            return ctx.enter_context(nc.semaphore(name))

        id_scratch = nc.dram_tensor("id_scratch", (NS, BATCH), fp16, kind="Internal").ap()

        ids = sb("ids", [P, TILES, FIELDS], i32)
        ids_h = sb("ids_h", [P, TILES, NS], fp16)
        id_dense_mem = sb("id_dense_mem", [32 + DIM, BATCH], f32)
        id_rows = id_dense_mem[0:NS, 0:BATCH // 2].bitcast(fp16)
        dense_t = id_dense_mem[32:32 + DIM, :]
        id_all = sb("id_all", [HI, ID_RING, GROUP, HALF], fp16)
        iota_i = sb("iota_i", [HI, 18], i32)
        iota_f = sb("iota_f", [HI, 18], f32)
        ident = sb("ident", [P, P], f32)
        ident_b = sb("ident_b", [P, P], bf16)
        ident_h = sb("ident_h", [P, P], fp16)
        gram_mem = sb("gram_mem", [P, FIELDS * P], f32)
        gram = gram_mem[0:FIELDS, :].rearrange("i (j b) -> i j b", b=P)
        tbl = gram_mem[0:HI, 0:LO_AT[NS] * DIM].rearrange("p (l d) -> p l d", d=DIM)
        keep = (LO_AT[NS] - PARTS_CUT) * K3 // 2
        w1_mem = sb("w1_mem", [P, keep + SLOTS * HIDDEN1], f32)
        w1 = w1_mem[:, keep:].rearrange("p (s n) -> p s n", n=HIDDEN1)
        tbl3 = w1_mem[0:HI, 0:LO_AT[NS] * K3 // 2].bitcast(bf16).rearrange("p (l k) -> p l k", k=K3)
        W1_AFTER_ONE = LO_AT[GROUPS[1][0]] * K3 // 2 // HIDDEN1
        W1_OVER = -(-(PARTS_CUT * K3 // 2) // HIDDEN1)
        onehot = sb("onehot", [HI, OH_RING, GROUP, HALF], bf16)
        emb = sb("emb", [P, 2, NB, DIM], f32)
        emb3 = sb("emb3", [P, NB, BLOCKS, DIM], bf16)
        lhs = sb("lhs", [BLOCKS * DIM, TILES, FIELDS, P], bf16)
        rhs = sb("rhs", [KG, TILES, FIELDS, P], bf16)
        z = sb("z", [P, 2, SLOTS, P], f32)
        dense = sb("dense", [P, TILES, DIM], f32)
        warm = sb("warm", [1, 2], f32)
        w2 = sb("w2", [P, HIDDEN1 // P, HIDDEN2], f32)
        vec = sb("vec", [8, P], f32)
        vec_t = sb("vec_t", [P, 8], f32)
        h1 = sb("h1", [P, HIDDEN1 // P, P], f32)
        h2 = sb("h2", [P, HIDDEN2 // P, P], f32)
        y = sb("y", [P, TILES], f32)

        banks = [pb(f"banks{i}", [P, 2, 512], f32) for i in range(2)]
        bank = [banks[i // 2][:, i % 2, :] for i in range(4)]
        ps_tr = [pb(f"ps_tr{i}", [P, TURN, P], bf16) for i in range(2)]
        ps_h1_even = pb("ps_h1_even", [P, HIDDEN1 // P, P], f32)
        ps_h1 = [ps_h1_even[:, :, :], bank[3].rearrange("p (c b) -> p c b", b=P)]
        ps_h2 = pb("ps_h2", [P, 512], f32)

        def h1_at(t, c):
            return ps_h1[t % 2][:, c, :] if t < TILES - 1 else bank[c][:, 0:P]

        gram_banks = [*bank[0:2], *(x[:, :, :].rearrange("p k b -> p (k b)").bitcast(f32) for x in ps_tr)]
        gram_bank = [gram_banks + [ps_h2[:, :] if t < 2 else bank[2]] for t in range(TILES)]
        ps_ids = ps_tr[0][0:NS, 0:TILES, :].bitcast(fp16)
        ps_dense = ps_h1_even[0:DIM, :, :]
        ps_vec = ps_h2[:, 0:8]

        ids_in = sem("ids_in")
        tbl_in = [sem(f"tbl_in{c}") for c in range(len(PIECES))]
        warm_ok = sem("warm_ok")
        w1_in, w2_in, vec_in, dense_in = sem("w1_in"), sem("w2_in"), sem("vec_in"), sem("dense_in")
        ident_zero, ident_ok, ident_b_ok = sem("ident_zero"), sem("ident_ok"), sem("ident_b_ok")
        ident_h_ok = sem("ident_h_ok")
        iota_ok, iota_f_ok = sem("iota_ok"), sem("iota_f_ok")
        ids_h_ok, ids_turned, id_rows_ok = sem("ids_h_ok"), sem("ids_turned"), sem("id_rows_ok")
        id_scratch_ok = sem("id_scratch_ok")
        id_all_in = [sem(f"id_all_in{i}") for i in range(ID_RING)]
        high_ok, rest_ok, mid_ok, tbl3_ok = sem("high_ok"), sem("rest_ok"), sem("mid_ok"), sem("tbl3_ok")
        onehot_ok, onehot_used = sem("onehot_ok"), sem("onehot_used")
        look_copied = sem("look_copied")
        rows_in = [[sem(f"rows_in{t}_{r}") for r in range(ROUNDS)] for t in range(TILES)]
        e_high, e_rest, e_mid, emb3_ok = sem("e_high"), sem("e_rest"), sem("e_mid"), sem("emb3_ok")
        turned, left_ok, right_ok = sem("turned"), sem("left_ok"), sem("right_ok")
        left_in = [sem(f"left_in{i}") for i in range(len(SPREADS))]
        right_in = [sem(f"right_in{i}") for i in range(len(SPREADS))]
        right_big_in = [sem(f"right_big_in{t}") for t in range(TILES - 1)]
        gram_ok = sem("gram_ok")
        gram_out_act, gram_out_dve = sem("gram_out_act"), sem("gram_out_dve")
        z_in = [sem(f"z_in{t}") for t in range(TILES)]
        z_in_pool = sem("z_in_pool")
        dense_z = [sem(f"dense_z{t}") for t in range(TILES)]
        dense_turned, dense_t_ok, vec_turned, vec_t_ok = (sem("dense_turned"), sem("dense_t_ok"),
                                                          sem("vec_turned"), sem("vec_t_ok"))
        layer1, h1_ok, layer2, h2_ok = sem("layer1"), sem("h1_ok"), sem("layer2"), sem("h2_ok")
        layer3, y_ok, out_ok = sem("layer3"), sem("y_ok"), sem("out_ok")

        POOL_MOVES = 4
        Z_COUNT = 16 * len(MOVES)

        def looked(n):
            return banks[n % 2][:, :, :].rearrange("p k (s b) -> p (k s) b", b=HALF)

        def splits(t, r):
            return t + 1 if t < TILES - 1 else TILES + r

        def samples(k):
            return slice(SPF * k, min(SPF * (k + 1), P))

        def filled(t, k):
            n = min(SPF, P - SPF * k)
            return gram_bank[t][k % GRAM_BANKS][0:FIELDS, 0:n * FIELDS].rearrange("i (b j) -> i j b", b=n)

        def move(eng, done, t, row, rows, slot, slots, i, j):
            eng.dma_start(z[row:row + rows, t % 2, slot:slot + slots, :],
                          gram[i:i + rows, j:j + slots, :]).then_inc(done, 16)

        left_copies = [(3 * DIM, HIGH_B * DIM, DIM), (4 * DIM, HIGH_B * DIM, DIM), (5 * DIM, MID_B * DIM, DIM)]
        right_copies = [(0, DIM, 5 * DIM), (5 * DIM, MID_B * DIM, DIM)]

        def load_tables(eng, g, first_table=0, last_table=GROUP):
            for s in range(*PIECES[g])[first_table:last_table]:
                eng.dma_start(tbl[:, LO_AT[s]:LO_AT[s + 1], :],
                              a[f"tbl_{SMALL[s]}"].rearrange("(p l) d -> p l d", l=LO[s])).then_inc(tbl_in[g], 16)

        def table_rows(g):
            return slice(LO_AT[PIECES[g][0]], LO_AT[PIECES[g][1]])

        def parts_at(s):
            return (LO_AT[s] - PARTS_CUT) % LO_AT[NS]

        def parts_rows(g):
            at = parts_at(PIECES[g][0])
            return slice(at, at + LO_AT[PIECES[g][1]] - LO_AT[PIECES[g][0]])

        block = ctx.enter_context(nc.Block())

        @block.sync
        def _(sp):
            sp.dma_start(ids[:, :, :], a["ids"].rearrange("(p t) f -> p t f", t=TILES)).then_inc(ids_in, 16)
            load_tables(sp, 0)
            load_tables(sp, 2, 0, 4)
            sp.wait_ge(id_scratch_ok, 16)

            def spread_ids(n):
                if n >= ID_RING:
                    sp.wait_ge(onehot_ok, LOOKS[n - ID_RING + 1])
                half, (s0, s1) = n // len(GROUPS), GROUPS[n % len(GROUPS)]
                src = id_scratch[s0:s1, HALF * half:HALF * (half + 1)].rearrange("(o f) b -> o f b", o=1)
                sp.dma_start(id_all[:, n % ID_RING, 0:s1 - s0, :],
                             src.broadcast_to((HI, s1 - s0, HALF))).then_inc(id_all_in[n % ID_RING], 16)

            spread_ids(0)
            load_tables(sp, 2, 4)
            spread_ids(1)
            load_tables(sp, 3)
            load_tables(sp, 4)
            sp.dma_start(vec[0:4, :], a["b_top1"].rearrange("(c p) -> c p", p=P)).then_inc(vec_in, 16)
            sp.dma_start(vec[4:6, :], a["b_top2"].rearrange("(c p) -> c p", p=P)).then_inc(vec_in, 16)
            sp.dma_start(vec[6:8, :], a["W_top3"].rearrange("(c p) n -> c (p n)", p=P)).then_inc(vec_in, 16)
            sp.dma_start(dense[:, :, :], a["dense_ctx"].rearrange("(p t) d -> p t d", t=TILES)).then_inc(dense_in, 16)
            sp.dma_start(w1[:, W1_OVER:, :], a["w1_slots"][:, W1_OVER:, :]).then_inc(w1_in, 16)
            spread_ids(2)
            sp.dma_start(w2[:, :, :], a["W_top2"].rearrange("(c p) n -> p c n", p=P)).then_inc(w2_in, 16)

            def dense_to_z(t):
                sp.dma_start(z[DENSE_AT:DENSE_AT + DIM, t % 2, DENSE_SLOT, :],
                             dense_t[:, t * P:(t + 1) * P]).then_inc(dense_z[t], 16)

            def spread_left(i):
                steps, half, s0, s1 = SPREADS[i]
                sp.wait_ge(look_copied, 2 * steps)
                tiles = slice(2 * half, 2 * half + 2)
                for row, src, rows in left_copies:
                    sp.dma_start(lhs[row:row + rows, tiles, s0:s1, :],
                                 lhs[src:src + rows, tiles, s0:s1, :]).then_inc(left_in[i], 16)

            def spread_right(i):
                steps, half, s0, s1 = SPREADS[i]
                tiles = slice(2 * half, 2 * half + 2)
                sp.wait_ge(left_in[i], 16 * len(left_copies))
                for row, src, rows in right_copies:
                    sp.dma_start(rhs[row:row + rows, tiles, s0:s1, :],
                                 lhs[src:src + rows, tiles, s0:s1, :]).then_inc(right_in[i], 16)

            def shift_big(t):
                sp.wait_ge(left_ok, ROUNDS * (t + 1))
                sp.dma_start(rhs[:, t, NS:, :], lhs[DIM:, t, NS:, :]).then_inc(right_big_in[t], 16)

            def fill_z(t, first_move=0, last_move=len(MOVES)):
                sp.wait_ge(gram_out_act, len(ACT_FILLS) * (t + 1))
                sp.wait_ge(gram_out_dve, len(DVE_FILLS) * (t + 1))
                for m in MOVES[first_move:last_move]:
                    move(sp, z_in[t], t, *m)

            spread_ids(3)
            spread_left(0)
            spread_ids(4)
            spread_right(0)
            spread_ids(5)
            spread_left(1)
            shift_big(0)
            spread_right(1)
            spread_ids(6)
            sp.wait_ge(dense_t_ok, 1)
            dense_to_z(0)
            dense_to_z(1)
            sp.wait_ge(onehot_used, LOOKS[len(GROUPS) + 1])
            sp.dma_start(w1[:, 0:W1_AFTER_ONE, :], a["w1_slots"][:, 0:W1_AFTER_ONE, :]).then_inc(w1_in, 16)
            fill_z(0, 0, 5)
            spread_ids(7)
            fill_z(0, 5, 8)
            sp.wait_ge(onehot_used, LOOKS[len(GROUPS) + GROUPS_CUT])
            sp.dma_start(w1[:, W1_AFTER_ONE:W1_OVER, :],
                         a["w1_slots"][:, W1_AFTER_ONE:W1_OVER, :]).then_inc(w1_in, 16)
            fill_z(0, 8)
            shift_big(1)
            spread_left(2)
            fill_z(1, 0, 4)
            spread_right(2)
            fill_z(1, 4)
            for t in range(2, TILES):
                if t < TILES - 1:
                    shift_big(t)
                sp.wait_ge(layer1, 4 * (t - 1))
                dense_to_z(t)
                fill_z(t, 0 if t < TILES - 1 else POOL_MOVES)
            sp.wait_ge(y_ok, TILES)
            sp.dma_start(out.rearrange("(p t) o -> p (t o)", t=TILES), y[:, :]).then_inc(out_ok, 16)
            sp.wait_ge(out_ok, 16)

        @block.gpsimd
        def _(pool):
            pool.memset(ident[:, :], 0.0).then_inc(ident_zero, 1)
            pool.iota(iota_i[:, 0:10], pattern=[[1, 10]], base=0, channel_multiplier=10)
            pool.iota(iota_i[:, 10:18], pattern=[[1, 8]], base=0, channel_multiplier=8).then_inc(iota_ok, 1)
            pool.wait_ge(ident_zero, 1)
            pool.affine_select(out=ident[:, :], in_=ident[:, :], compare_op=ALU.not_equal, fill=1.0, base=0,
                               pattern=[[-1, P]], channel_multiplier=1).then_inc(ident_ok, 1)
            pool.wait_ge(ids_in, 16)
            for t in range(TILES):
                if t >= 2:
                    pool.wait_ge(emb3_ok, t - 1)
                for k, f in enumerate(BIG):
                    pool.indirect_dma_start(
                        out=emb[:, t % 2, k, :], out_offset=None, in_=a[f"tbl_{f}"],
                        in_offset=bass.IndirectOffsetOnAxis(ap=ids[:, t, NS + k:NS + k + 1], axis=0),
                    ).then_inc(rows_in[t][k // TURN], 16)
            pool.wait_ge(layer1, 4 * (TILES - 2))
            pool.wait_ge(gram_out_act, len(ACT_FILLS) * TILES)
            pool.wait_ge(gram_out_dve, len(DVE_FILLS) * TILES)
            for m in MOVES[:POOL_MOVES]:
                move(pool, z_in_pool, TILES - 1, *m)

        @block.scalar
        def _(act):
            act.wait_ge(warm_ok, 1)
            act.activation(warm[:, 1:2], warm[:, 0:1], ACT.Copy)
            load_tables(act, 1)
            act.wait_ge(id_rows_ok, 1)
            act.dma_start(id_scratch, id_rows).then_inc(id_scratch_ok, 16)

            def high_part(g):
                act.wait_ge(tbl_in[g], 16 * (PIECES[g][1] - PIECES[g][0]))
                act.activation(tbl3[:, parts_rows(g), HIGH_B * DIM:(HIGH_B + 1) * DIM], tbl[:, table_rows(g), :],
                               ACT.Copy).then_inc(high_ok, 1)

            def middle_part(g):
                act.wait_ge(rest_ok, g + 1)
                act.activation(tbl3[:, parts_rows(g), MID_B * DIM:(MID_B + 1) * DIM], tbl[:, table_rows(g), :],
                               ACT.Copy).then_inc(mid_ok, 1)

            def copy_looked(n):
                act.wait_ge(onehot_used, LOOKS[n + 1])
                half, (s0, s1) = n // len(GROUPS), GROUPS[n % len(GROUPS)]
                for side in range(2):
                    tables = (s1 - s0 - side + 1) // 2
                    act.activation(lhs[0:K3, 2 * half:2 * half + 2, s0 + side:s1:2, :].rearrange("k t s p -> k s t p"),
                                   looked(n)[64 * side:64 * side + K3, 0:tables, :]
                                   .rearrange("k s (t p) -> k s t p", p=P), ACT.Copy).then_inc(look_copied, 1)

            def copy_turned(t, r):
                act.wait_ge(turned, ROUNDS * t + r + 1)
                rows, bank_at = (BLOCKS * DIM, r % 2) if t < TILES - 1 else (KG, 0)
                act.activation(lhs[0:rows, t, NS + TURN * r:NS + TURN * (r + 1), :],
                               ps_tr[bank_at][0:rows, :, :], ACT.Copy).then_inc(left_ok, 1)

            def gram_out(t):
                if t >= 1:
                    act.wait_ge(z_in[t - 1], Z_COUNT)
                for k in ACT_FILLS:
                    act.wait_ge(gram_ok, FILLS * t + k + 1)
                    act.activation(gram[:, :, samples(k)], filled(t, k), ACT.Copy).then_inc(gram_out_act, 1)

            high_part(0)
            high_part(1)
            middle_part(0)
            middle_part(1)
            high_part(2)
            for n in range(len(GROUPS)):
                if n >= 1:
                    copy_looked(n - 1)
                if n + 2 < len(PIECES):
                    middle_part(n + 2)
                if n + 3 < len(PIECES):
                    high_part(n + 3)
            copy_turned(0, 0)
            copy_looked(3)
            copy_turned(0, 1)
            copy_turned(0, 2)
            copy_looked(4)
            gram_out(0)
            copy_looked(5)
            copy_turned(1, 0)
            copy_turned(1, 1)
            copy_looked(6)
            copy_turned(1, 2)
            copy_looked(7)
            gram_out(1)
            for t in (2, 3):
                for r in range(ROUNDS):
                    copy_turned(t, r)
                gram_out(t)

        @block.vector
        def _(dve):
            dve.memset(warm[:, 0:1], 0.0).then_inc(warm_ok, 1)
            dve.wait_ge(ident_ok, 1)
            dve.tensor_copy(ident_h[:, :], ident[:, :]).then_inc(ident_h_ok, 1)
            dve.wait_ge(ids_in, 16)
            dve.tensor_copy(ids_h[:, :, :], ids[:, :, 0:NS]).then_inc(ids_h_ok, 1)
            dve.tensor_copy(ident_b[:, :], ident[:, :]).then_inc(ident_b_ok, 1)
            dve.wait_ge(iota_ok, 1)
            dve.tensor_copy(iota_f[:, :], iota_i[:, :]).then_inc(iota_f_ok, 1)
            dve.wait_ge(ids_turned, 1)
            dve.tensor_copy(id_rows.rearrange("f (t p) -> f t p", p=P), ps_ids).then_inc(id_rows_ok, 1)

            def copy_dense_vec():
                dve.wait_ge(dense_turned, 1)
                dve.tensor_copy(dense_t.rearrange("d (t p) -> d t p", p=P), ps_dense).then_inc(dense_t_ok, 1)
                dve.wait_ge(vec_turned, 1)
                dve.tensor_copy(vec_t[:, :], ps_vec).then_inc(vec_t_ok, 1)

            def rest(g):
                dve.wait_ge(high_ok, g + 1)
                dve.tensor_tensor(tbl[:, table_rows(g), :], tbl[:, table_rows(g), :],
                                  tbl3[:, parts_rows(g), HIGH_B * DIM:(HIGH_B + 1) * DIM],
                                  ALU.subtract).then_inc(rest_ok, 1)

            def low_part(g):
                dve.wait_ge(mid_ok, g + 1)
                dve.tensor_tensor(tbl3[:, parts_rows(g), LOW_B * DIM:(LOW_B + 1) * DIM], tbl[:, table_rows(g), :],
                                  tbl3[:, parts_rows(g), MID_B * DIM:(MID_B + 1) * DIM],
                                  ALU.subtract).then_inc(tbl3_ok, 1)

            def fields_of(t, r):
                k = slice(0, NB) if t < TILES - 1 else slice(TURN * r, TURN * (r + 1))
                e = emb[:, t % 2, k, :]
                n = NB if t < TILES - 1 else TURN
                return e, e.rearrange("p f (o d) -> p f o d", o=1).broadcast_to((P, n, 2, DIM)), emb3[:, k, :, :]

            def split_high(t, r=ROUNDS - 1):
                e, twice, e3 = fields_of(t, r)
                for q in (range(ROUNDS) if t < TILES - 1 else [r]):
                    dve.wait_ge(rows_in[t][q], 16 * TURN)
                if t >= 1:
                    dve.wait_ge(turned, ROUNDS * (t - 1) + r + 1)
                dve.tensor_copy(e3[:, :, 3:5, :], twice).then_inc(e_high, 1)
                dve.wait_ge(e_high, splits(t, r))
                dve.tensor_copy(e3[:, :, HIGH_B, :], e3[:, :, 3, :])
                dve.tensor_tensor(e, e, e3[:, :, 3, :], ALU.subtract).then_inc(e_rest, 1)

            def split_rest(t, r=ROUNDS - 1):
                e, twice, e3 = fields_of(t, r)
                dve.wait_ge(e_rest, splits(t, r))
                dve.tensor_copy(e3[:, :, 5:7, :], twice).then_inc(e_mid, 1)
                dve.wait_ge(e_mid, splits(t, r))
                dve.tensor_copy(e3[:, :, MID_B, :], e3[:, :, 5, :])
                dve.tensor_tensor(e3[:, :, LOW_B, :], e, e3[:, :, 5, :], ALU.subtract).then_inc(emb3_ok, 1)

            def copy_right(r):
                dve.wait_ge(turned, ROUNDS * (TILES - 1) + r + 1)
                dve.tensor_copy(rhs[:, TILES - 1, NS + TURN * r:NS + TURN * (r + 1), :],
                                ps_tr[1][0:KG, :, :]).then_inc(right_ok, 1)

            def compare(n, first_lo=0, last_lo=None):
                half, g = n // len(GROUPS), n % len(GROUPS)
                s0, s1 = GROUPS[g]
                dve.wait_ge(id_all_in[n % ID_RING], 16 * (n // ID_RING + 1))
                base = 0 if LO[s0] == 10 else 10
                for lo in range(LO[s0])[first_lo:last_lo]:
                    c = LOOKS[n] + lo
                    if c >= OH_RING:
                        dve.wait_ge(onehot_used, c - OH_RING + 1)
                    dve.tensor_scalar(onehot[:, c % OH_RING, 0:s1 - s0, :], id_all[:, n % ID_RING, 0:s1 - s0, :],
                                      iota_f[:, base + lo:base + lo + 1], None, ALU.is_equal).then_inc(onehot_ok, 1)
                    if lo == 4 and n + 2 < len(PIECES):
                        rest(n + 2)
                if n + 2 < len(PIECES):
                    low_part(n + 2)

            def gram_out(t):
                if t >= 1:
                    dve.wait_ge(z_in[t - 1], Z_COUNT)
                for k in DVE_FILLS:
                    dve.wait_ge(gram_ok, FILLS * t + k + 1)
                    dve.tensor_copy(gram[:, :, samples(k)], filled(t, k)).then_inc(gram_out_dve, 1)

            def relu1(t):
                if t >= 1:
                    dve.wait_ge(layer2, t)
                for c in range(HIDDEN1 // P):
                    dve.wait_ge(layer1, 4 * t + (c + 1 if t == TILES - 1 else 4))
                    dve.tensor_scalar(h1[:, c, :], h1_at(t, c), vec_t[:, c:c + 1], 0.0, ALU.add, ALU.max
                                      ).then_inc(h1_ok, 1)

            def relu2(t):
                dve.wait_ge(layer2, t + 1)
                if t >= 1:
                    dve.wait_ge(layer3, t)
                for c in range(HIDDEN2 // P):
                    dve.tensor_scalar(h2[:, c, :], ps_h2[:, c * P:(c + 1) * P], vec_t[:, 4 + c:5 + c], 0.0,
                                      ALU.add, ALU.max).then_inc(h2_ok, 1)

            def copy_y(t):
                dve.wait_ge(layer3, t + 1)
                dve.tensor_copy(y[:, t:t + 1], ps_h2[:, 2 * P:2 * P + 1]).then_inc(y_ok, 1)

            dve.wait_ge(iota_f_ok, 1)
            rest(0)
            rest(1)
            low_part(0)
            low_part(1)
            compare(0)
            compare(1)
            compare(2)
            copy_dense_vec()
            compare(3, 0, 2)
            split_high(0)
            compare(3, 2, 4)
            split_rest(0)
            compare(3, 4)
            compare(4)
            compare(5, 0, 8)
            gram_out(0)
            compare(5, 8)
            compare(6, 0, 1)
            split_high(1)
            compare(6, 1, 3)
            split_rest(1)
            compare(6, 3)
            compare(7)
            gram_out(1)
            split_high(2)
            split_rest(2)
            relu1(0)
            relu2(0)
            split_high(3, 0)
            split_rest(3, 0)
            copy_y(0)
            gram_out(2)
            copy_right(0)
            split_high(3, 1)
            split_rest(3, 1)
            relu1(1)
            copy_right(1)
            split_high(3, 2)
            split_rest(3, 2)
            relu2(1)
            copy_right(2)
            copy_y(1)
            gram_out(3)
            relu1(2)
            relu2(2)
            copy_y(2)
            relu1(3)
            relu2(3)
            copy_y(3)

        @block.tensor
        def _(pe):
            pe.wait_ge(ident_h_ok, 1)
            pe.wait_ge(ids_h_ok, 1)
            for t in range(TILES):
                last = pe.transpose(ps_ids[:, t, :], ids_h[:, t, :], ident_h[:, :])
            last.then_inc(ids_turned, 1)
            pe.wait_ge(ident_b_ok, 1)
            pe.wait_ge(id_rows_ok, 1)

            def turn_dense_vec():
                pe.wait_ge(dense_in, 16)
                for t in range(TILES):
                    last = pe.transpose(ps_dense[:, t, :], dense[:, t, :], ident[:, :])
                last.then_inc(dense_turned, 1)
                pe.wait_ge(vec_in, 48)
                pe.transpose(ps_vec, vec[:, :], ident[0:8, 0:8]).then_inc(vec_turned, 1)

            def turn(t, r):
                pe.wait_ge(emb3_ok, splits(t, r))
                n = ROUNDS * t + r
                e3 = emb3[:, :, :, :].rearrange("p f k d -> p f (k d)")
                if t < TILES - 1:
                    if n >= 1:
                        pe.wait_ge(left_ok, n - 1 if r > 0 else n)
                    for k in range(TURN):
                        last = pe.transpose(ps_tr[r % 2][0:BLOCKS * DIM, k, :], e3[:, TURN * r + k, :], ident_b[:, :])
                else:
                    pe.wait_ge(left_ok, n)
                    if r > 0:
                        pe.wait_ge(right_ok, r)
                    for side in range(2):
                        for k in range(TURN):
                            last = pe.transpose(ps_tr[side][0:KG, k, :],
                                                e3[:, TURN * r + k, DIM * side:DIM * side + KG], ident_b[:, :])
                last.then_inc(turned, 1)

            def look(n, first_lo=0, last_lo=None):
                s0, s1 = GROUPS[n % len(GROUPS)]
                pe.wait_ge(tbl3_ok, n % len(GROUPS) + 2)
                if n >= 2:
                    pe.wait_ge(look_copied, 2 * (n - 1))
                for lo in range(LO[s0])[first_lo:last_lo]:
                    c = LOOKS[n] + lo
                    pe.wait_ge(onehot_ok, c + 1)
                    for s in range(s0, s1):
                        e, side = (s - s0) // 2, (s - s0) % 2
                        last = pe.matmul(looked(n)[64 * side:64 * side + K3, e, :],
                                         lhsT=tbl3[:, parts_at(s) + lo, :], rhs=onehot[:, c % OH_RING, s - s0, :],
                                         start=lo == 0 and e % 2 == 0,
                                         stop=lo == LO[s0] - 1 and (e % 2 == 1 or s >= s1 - 2))
                    last.then_inc(onehot_used, 1)

            def gram_banks_free(tiles):
                pe.wait_ge(gram_out_dve, len(DVE_FILLS) * tiles)
                pe.wait_ge(gram_out_act, len(ACT_FILLS) * tiles)

            def operands_in(t):
                pe.wait_ge(z_in[t], Z_COUNT if t < TILES - 1 else Z_COUNT - 16 * POOL_MOVES)
                if t == TILES - 1:
                    pe.wait_ge(z_in_pool, 16 * POOL_MOVES)
                    gram_banks_free(TILES)
                pe.wait_ge(dense_z[t], 16)
                pe.wait_ge(w1_in, 48)
                if t >= 2:
                    pe.wait_ge(h1_ok, 4 * (t - 1))

            def product(t, c, s):
                r = SLOT_ROWS[s]
                done = pe.matmul(h1_at(t, c), lhsT=w1[0:r, s, c * P:(c + 1) * P], rhs=z[0:r, t % 2, s, :],
                                 start=s == 0, stop=s == SLOTS - 1)
                if s == SLOTS - 1:
                    done.then_inc(layer1, 1)

            def first(t, chunks):
                if 0 in chunks:
                    operands_in(t)
                for c in chunks:
                    for s in range(SLOTS):
                        product(t, c, s)

            def gram_tile(t, looked):
                for i, (_, half, _, _) in enumerate(SPREADS):
                    if half == t // 2:
                        pe.wait_ge(left_in[i], 16 * len(left_copies))
                        pe.wait_ge(right_in[i], 16 * len(right_copies))
                pe.wait_ge(left_ok, ROUNDS * (t + 1))
                if t < TILES - 1:
                    pe.wait_ge(right_big_in[t], 16)
                else:
                    pe.wait_ge(right_ok, ROUNDS)
                pe.wait_ge(look_copied, 2 * looked)
                gram_banks_free(t)
                for k in range(FILLS):
                    k0 = k - GRAM_BANKS
                    if k0 in DVE_FILLS:
                        pe.wait_ge(gram_out_dve, len(DVE_FILLS) * t + DVE_FILLS.index(k0) + 1)
                    elif k0 in ACT_FILLS:
                        pe.wait_ge(gram_out_act, len(ACT_FILLS) * t + ACT_FILLS.index(k0) + 1)
                    for n, b in enumerate(range(SPF * k, min(SPF * (k + 1), P))):
                        last = pe.matmul(gram_bank[t][k % GRAM_BANKS][0:FIELDS, n * FIELDS:(n + 1) * FIELDS],
                                         lhsT=lhs[0:KG, t, :, b], rhs=rhs[:, t, :, b], start=True, stop=True)
                    last.then_inc(gram_ok, 1)

            def second(t):
                pe.wait_ge(h1_ok, 4 * (t + 1))
                pe.wait_ge(w2_in, 16)
                if t == 0:
                    pe.wait_ge(vec_t_ok, 1)
                else:
                    pe.wait_ge(y_ok, t)
                for c in range(HIDDEN2 // P):
                    for k in range(HIDDEN1 // P):
                        last = pe.matmul(ps_h2[:, c * P:(c + 1) * P], lhsT=w2[:, k, c * P:(c + 1) * P],
                                         rhs=h1[:, k, :], start=k == 0, stop=k == HIDDEN1 // P - 1)
                last.then_inc(layer2, 1)

            def third(t):
                pe.wait_ge(h2_ok, 2 * (t + 1))
                for c in range(HIDDEN2 // P):
                    last = pe.matmul(ps_h2[:, 2 * P:2 * P + 1], lhsT=h2[:, c, :], rhs=vec_t[:, 6 + c:7 + c],
                                     start=c == 0, stop=c == HIDDEN2 // P - 1)
                last.then_inc(layer3, 1)

            look(0)
            look(1)
            turn_dense_vec()
            look(2)
            look(3, 0, 6)
            turn(0, 0)
            look(3, 6)
            turn(0, 1)
            look(4, 0, 4)
            turn(0, 2)
            look(4, 4)
            look(5, 0, 5)
            gram_tile(0, 5)
            look(5, 5)
            gram_banks_free(1)
            look(6, 0, 3)
            turn(1, 0)
            turn(1, 1)
            look(6, 3)
            turn(1, 2)
            look(7)
            first(0, [0])
            gram_tile(1, STEPS)
            first(0, [1, 2, 3])
            gram_banks_free(2)
            turn(2, 0)
            turn(2, 1)
            turn(2, 2)
            second(0)
            first(1, [0])
            third(0)
            gram_tile(2, STEPS)
            first(1, [1])
            gram_banks_free(3)
            turn(3, 0)
            first(1, [2, 3])
            turn(3, 1)
            second(1)
            turn(3, 2)
            first(2, [0])
            third(1)
            gram_tile(3, STEPS)
            first(2, [1])
            first(2, [2, 3])
            first(3, [0])
            second(2)
            first(3, [1])
            third(2)
            first(3, [2, 3])
            second(3)
            third(3)


def slot_rows():
    def pair(i, j):
        x, y = sorted((ORDER[i], ORDER[j]))
        return x * FIELDS - x * (x + 1) // 2 + y - x - 1

    where, placed = [], set()
    for row, rows, slot, slots, i, j in MOVES:
        for r in range(rows):
            for c in range(slots):
                if i + r < j + c and (i + r, j + c) not in placed:
                    placed.add((i + r, j + c))
                    where.append((slot + c, row + r, pair(i + r, j + c)))
    assert len(placed) == FIELDS * (FIELDS - 1) // 2
    return where + [(DENSE_SLOT, DENSE_AT + d, FIELDS * (FIELDS - 1) // 2 + d) for d in range(DIM)]


_INS = ["dense_ctx", "ids"] + [f"tbl_{f}" for f in range(FIELDS)] + ["w1_slots", "b_top1", "W_top2", "b_top2", "W_top3"]


def kernel(**inputs):
    import numpy as _np
    import concourse.bacc as _bacc
    from concourse import mybir as _mybir
    from concourse.bass_utils import run_bass_kernel_spmd as _run

    given = {name: _np.asarray(x) for name, x in inputs.items()}
    given["ids"] = given["ids"][:, ORDER]
    w1 = given["W_top1"]
    slots = _np.zeros((P, SLOTS, HIDDEN1), w1.dtype)
    where = _np.array(slot_rows())
    slots[where[:, 1], where[:, 0]] = w1[where[:, 2]]
    given["w1_slots"] = slots

    nc = _bacc.Bacc("TRN2", target_bir_lowering=False, num_devices=1)
    arrays, aps = {}, {}
    for name in _INS:
        x = _np.ascontiguousarray(given[name])
        arrays[f"in_{name}"] = x
        aps[name] = nc.dram_tensor(f"in_{name}", x.shape, _mybir.dt.from_np(x.dtype), kind="ExternalInput").ap()
    out = nc.dram_tensor("out_0", (BATCH, 1), _mybir.dt.float32, kind="ExternalOutput").ap()
    dlrm_tower(nc, aps, out)
    r = _run(nc, [arrays], core_ids=[0])
    return r.results[0]["out_0"]
```
